# Optimizing a Trainium2 kernel written in Bass

```python
import numpy as np
import jax
import jax.numpy as jnp

def _softmax(x, axis=-1):
    return jax.nn.softmax(x, axis=axis)

def _gelu(x):
    return jax.nn.gelu(x, approximate=True)

def _silu(x):
    return jax.nn.silu(x)

def _sigmoid(x):
    return jax.nn.sigmoid(x)

def _layernorm(x, axis=-1, eps=1e-05):
    m = jnp.mean(x, axis=axis, keepdims=True)
    v = jnp.var(x, axis=axis, keepdims=True)
    return (x - m) / jnp.sqrt(v + eps)

def _scatter_add(tgt, idx, src, axis=0):
    return tgt.at[idx].add(src)

def _segment_sum(src, seg, n):
    return jax.ops.segment_sum(src, seg, n)
kernel_name = 'mk_audio_tower_d1_tok_audfeat256_r4_b8ccdb'

def setup_inputs(seed: int=0):
    np.random.seed(seed)
    _w = jnp.asarray

    def _rec_inputs():
        import jax
        import jax.numpy as jnp
        _rk = jax.random.key(seed)
        x = -0.000520686 + 1.00062 * jax.random.normal(jax.random.fold_in(_rk, 1), (128, 375, 64), jnp.float32)
        return x
    x = _rec_inputs()

    def _L0_tok_setup():
        import jax, jax.numpy as jnp
        import numpy as np
        BATCH = 2
        SEQ = 1024
        D_MODEL = 64
        N_STATE = 64
        DT_RANK = 1
        NUM_LAYERS = 3

        def _ssm_layer(x, A_log, Dp, W_dbc, W_dt, b_dt):
            A = -jnp.exp(A_log)
            dbc = jnp.einsum('ble,ce->blc', x, W_dbc)
            delta, Bm, Cm = jnp.split(dbc, [DT_RANK, DT_RANK + N_STATE], axis=-1)
            delta = jax.nn.softplus(jnp.einsum('blr,er->ble', delta, W_dt) + b_dt)
            dA = jnp.exp(delta[..., None] * A)
            dBx = (delta * x)[..., None] * Bm[:, :, None, :]

            def combine(c1, c2):
                a1, h1 = c1
                a2, h2 = c2
                return (a1 * a2, h1 * a2 + h2)
            _, hs = jax.lax.associative_scan(combine, (dA, dBx), axis=1)
            y = jnp.einsum('blen,bln->ble', hs, Cm)
            return y + Dp * x
        key = jax.random.key(seed)
        kx, kw1, kw2 = jax.random.split(key, 3)
        x = jax.random.normal(kx, (BATCH, SEQ, D_MODEL), dtype=jnp.float32)
        A_log = jnp.broadcast_to(jnp.log(jnp.arange(1, N_STATE + 1, dtype=jnp.float32)), (NUM_LAYERS, D_MODEL, N_STATE)).copy()
        D = jnp.ones((NUM_LAYERS, D_MODEL), dtype=jnp.float32)
        W_dbc = 0.02 * jax.random.normal(kw1, (NUM_LAYERS, DT_RANK + 2 * N_STATE, D_MODEL), dtype=jnp.float32)
        W_dt = 0.02 * jax.random.normal(kw2, (NUM_LAYERS, D_MODEL, DT_RANK), dtype=jnp.float32)
        b_dt = jnp.zeros((NUM_LAYERS, D_MODEL), dtype=jnp.float32)
        return {'x': x, 'A_log': A_log, 'D': D, 'W_dbc': W_dbc, 'W_dt': W_dt, 'b_dt': b_dt}
    _L0_tok_all = _L0_tok_setup()
    _L0_tok_in = {k: v for k, v in _L0_tok_all.items() if k in ('A_log', 'D', 'W_dbc', 'W_dt', 'b_dt')}
    del _L0_tok_all

    def _L0_attn_setup():
        import jax, jax.numpy as jnp
        import numpy as np
        A, Bc, Cc = (0.5, 1.0, 1.0)
        H = 8
        EPS = 1e-12

        def _normalize(t):
            n = jnp.linalg.norm(t, axis=-1, keepdims=True)
            return t / jnp.maximum(n, EPS)
        key = jax.random.key(seed)
        ks = jax.random.split(key, 5)
        B, N, C = (8, 512, 64)
        D = C // H
        x = jax.random.normal(ks[0], (B, N, C), dtype=jnp.float32)
        Wqkv = jax.random.normal(ks[1], (3 * H * D, C), dtype=jnp.float32) * 0.02
        bqkv = jnp.zeros((3 * H * D,), dtype=jnp.float32)
        Wproj = jax.random.normal(ks[2], (C, H * D), dtype=jnp.float32) * 0.02
        bproj = jnp.zeros((C,), dtype=jnp.float32)
        temperature = jnp.ones((1, H, 1, 1), dtype=jnp.float32)
        return {'x': x, 'Wqkv': Wqkv, 'bqkv': bqkv, 'Wproj': Wproj, 'bproj': bproj, 'temperature': temperature}
    _L0_attn_all = _L0_attn_setup()
    _L0_attn_in = {k: v for k, v in _L0_attn_all.items() if k in ('Wqkv', 'bqkv', 'Wproj', 'bproj', 'temperature')}
    del _L0_attn_all

    def _L0_ffn_setup():
        import jax, jax.numpy as jnp
        import numpy as np
        E, D, H, TOP_K = (6, 64, 64, 2)
        ROUTER_H = D // 2
        key = jax.random.key(seed)
        ks = jax.random.split(key, 12)
        s = 1.0 / np.sqrt(D)
        sh = 1.0 / np.sqrt(H)
        sr = 1.0 / np.sqrt(ROUTER_H)
        return {'features': jax.random.normal(ks[0], (8, 1024, D), dtype=jnp.float32), 'router_w1': jax.random.uniform(ks[1], (D, ROUTER_H), jnp.float32, -s, s), 'router_b1': jnp.zeros((ROUTER_H,), jnp.float32), 'router_w2': jax.random.uniform(ks[2], (ROUTER_H, E), jnp.float32, -sr, sr), 'router_b2': jnp.zeros((E,), jnp.float32), 'expert_w1': jax.random.uniform(ks[3], (E, D, H), jnp.float32, -s, s), 'expert_b1': jnp.zeros((E, H), jnp.float32), 'expert_w2': jax.random.uniform(ks[4], (E, H, H), jnp.float32, -sh, sh), 'expert_b2': jnp.zeros((E, H), jnp.float32), 'expert_w3': jax.random.uniform(ks[5], (E, H, D), jnp.float32, -sh, sh), 'expert_b3': jnp.zeros((E, D), jnp.float32)}
    _L0_ffn_all = _L0_ffn_setup()
    _L0_ffn_in = {k: v for k, v in _L0_ffn_all.items() if k in ('router_w1', 'router_b1', 'router_w2', 'router_b2', 'expert_w1', 'expert_b1', 'expert_w2', 'expert_b2', 'expert_w3', 'expert_b3')}
    del _L0_ffn_all
    return {'x': x, 'L0_tok_A_log': _L0_tok_in['A_log'], 'L0_tok_D': _L0_tok_in['D'], 'L0_tok_W_dbc': _L0_tok_in['W_dbc'], 'L0_tok_W_dt': _L0_tok_in['W_dt'], 'L0_tok_b_dt': _L0_tok_in['b_dt'], 'L0_attn_Wqkv': _L0_attn_in['Wqkv'], 'L0_attn_bqkv': _L0_attn_in['bqkv'], 'L0_attn_Wproj': _L0_attn_in['Wproj'], 'L0_attn_bproj': _L0_attn_in['bproj'], 'L0_attn_temperature': _L0_attn_in['temperature'], 'L0_ffn_router_w1': _L0_ffn_in['router_w1'], 'L0_ffn_router_b1': _L0_ffn_in['router_b1'], 'L0_ffn_router_w2': _L0_ffn_in['router_w2'], 'L0_ffn_router_b2': _L0_ffn_in['router_b2'], 'L0_ffn_expert_w1': _L0_ffn_in['expert_w1'], 'L0_ffn_expert_b1': _L0_ffn_in['expert_b1'], 'L0_ffn_expert_w2': _L0_ffn_in['expert_w2'], 'L0_ffn_expert_b2': _L0_ffn_in['expert_b2'], 'L0_ffn_expert_w3': _L0_ffn_in['expert_w3'], 'L0_ffn_expert_b3': _L0_ffn_in['expert_b3']}

def reference(x, L0_tok_A_log, L0_tok_D, L0_tok_W_dbc, L0_tok_W_dt, L0_tok_b_dt, L0_attn_Wqkv, L0_attn_bqkv, L0_attn_Wproj, L0_attn_bproj, L0_attn_temperature, L0_ffn_router_w1, L0_ffn_router_b1, L0_ffn_router_w2, L0_ffn_router_b2, L0_ffn_expert_w1, L0_ffn_expert_b1, L0_ffn_expert_w2, L0_ffn_expert_b2, L0_ffn_expert_w3, L0_ffn_expert_b3):
    import jax
    import jax.numpy as jnp

    def _L0_tok_ref(x, A_log, D, W_dbc, W_dt, b_dt):
        import jax, jax.numpy as jnp
        import numpy as np
        BATCH = 2
        SEQ = 1024
        D_MODEL = 64
        N_STATE = 64
        DT_RANK = 1
        NUM_LAYERS = 3

        def _ssm_layer(x, A_log, Dp, W_dbc, W_dt, b_dt):
            A = -jnp.exp(A_log)
            dbc = jnp.einsum('ble,ce->blc', x, W_dbc)
            delta, Bm, Cm = jnp.split(dbc, [DT_RANK, DT_RANK + N_STATE], axis=-1)
            delta = jax.nn.softplus(jnp.einsum('blr,er->ble', delta, W_dt) + b_dt)
            dA = jnp.exp(delta[..., None] * A)
            dBx = (delta * x)[..., None] * Bm[:, :, None, :]

            def combine(c1, c2):
                a1, h1 = c1
                a2, h2 = c2
                return (a1 * a2, h1 * a2 + h2)
            _, hs = jax.lax.associative_scan(combine, (dA, dBx), axis=1)
            y = jnp.einsum('blen,bln->ble', hs, Cm)
            return y + Dp * x
        for i in range(NUM_LAYERS):
            x = _ssm_layer(x, A_log[i], D[i], W_dbc[i], W_dt[i], b_dt[i])
            if i < NUM_LAYERS - 1:
                b, l, d = x.shape
                x = x[:, :l // 2 * 2].reshape(b, l // 2, 2, d).mean(axis=2)
        return x

    def _L0_attn_ref(x, Wqkv, bqkv, Wproj, bproj, temperature):
        import jax, jax.numpy as jnp
        import numpy as np
        A, Bc, Cc = (0.5, 1.0, 1.0)
        H = 8
        EPS = 1e-12

        def _normalize(t):
            n = jnp.linalg.norm(t, axis=-1, keepdims=True)
            return t / jnp.maximum(n, EPS)
        B, N, C = x.shape
        D = C // H
        scale = float(D) ** 0.25
        qkv = (x @ Wqkv.T + bqkv).reshape(B, N, 3, H, D)
        qkv = jnp.transpose(qkv, (2, 0, 3, 1, 4))
        q, k, v = (qkv[0], qkv[1], qkv[2])
        q = q * scale
        v1 = jnp.concatenate([jnp.ones((B, H, N, 1), dtype=v.dtype), v], axis=-1)
        qn = _normalize(q) * (scale * temperature)
        kn = _normalize(k) * scale
        vN = v1 / N
        kv_mod = jnp.einsum('bhni,bhnj,bhne->bhije', kn, kn, vN)
        kv = jnp.einsum('bhnd,bhne->bhde', kn, vN)
        vsum = jnp.sum(vN, axis=-2)[:, :, None, :]
        y = A * jnp.einsum('bhni,bhnj,bhije->bhne', qn, qn, kv_mod) + scale ** 2 * Bc * jnp.einsum('bhnd,bhde->bhne', qn, kv) + scale ** 4 * Cc * vsum
        y_norm, y = (y[..., :1], y[..., 1:])
        y = y / y_norm
        out = jnp.transpose(y, (0, 2, 1, 3)).reshape(B, N, H * D)
        return out @ Wproj.T + bproj

    def _L0_ffn_ref(features, router_w1, router_b1, router_w2, router_b2, expert_w1, expert_b1, expert_w2, expert_b2, expert_w3, expert_b3):
        import jax, jax.numpy as jnp
        import numpy as np
        E, D, H, TOP_K = (6, 64, 64, 2)
        ROUTER_H = D // 2
        rh = jax.nn.relu(features @ router_w1 + router_b1)
        expert_logits = jax.nn.softmax(rh @ router_w2 + router_b2, axis=-1)
        top_w, top_i = jax.lax.top_k(expert_logits, TOP_K)
        routing_weights = jax.nn.softmax(top_w, axis=-1)
        h1 = jax.nn.relu(jnp.einsum('bsd,edh->bseh', features, expert_w1) + expert_b1)
        h2 = jax.nn.relu(jnp.einsum('bseh,ehf->bsef', h1, expert_w2) + expert_b2)
        expert_out = jnp.einsum('bsef,efo->bseo', h2, expert_w3) + expert_b3
        sel = jnp.take_along_axis(expert_out, top_i[:, :, :, None], axis=2)
        combined = jnp.sum(sel * routing_weights[..., None], axis=2)
        return combined
    h = _L0_tok_ref(x, L0_tok_A_log, L0_tok_D, L0_tok_W_dbc, L0_tok_W_dt, L0_tok_b_dt)
    h = h + _L0_attn_ref(_layernorm(h, axis=-1), L0_attn_Wqkv, L0_attn_bqkv, L0_attn_Wproj, L0_attn_bproj, L0_attn_temperature)
    h = h + _L0_ffn_ref(_layernorm(h, axis=-1), L0_ffn_router_w1, L0_ffn_router_b1, L0_ffn_router_w2, L0_ffn_router_b2, L0_ffn_expert_w1, L0_ffn_expert_b1, L0_ffn_expert_w2, L0_ffn_expert_b2, L0_ffn_expert_w3, L0_ffn_expert_b3)
    return h

_drawn_inputs = setup_inputs


def setup_inputs(seed=0):
    import zlib

    import numpy as np

    out = dict(_drawn_inputs(seed))
    spreads = {'L0_tok_D': (1.0, 0.2),
     'L0_tok_b_dt': (0.0, 0.362),
     'L0_attn_bqkv': (0.0, 0.1),
     'L0_attn_bproj': (0.0, 0.1),
     'L0_attn_temperature': (1.0, 0.6),
     'L0_ffn_router_b1': (0.0, 0.1),
     'L0_ffn_router_b2': (0.0, 0.1),
     'L0_ffn_expert_b1': (0.0, 0.379),
     'L0_ffn_expert_b2': (0.0, 0.1),
     'L0_ffn_expert_b3': (0.0, 0.1)}
    factors = {'L0_tok_A_log': 9.516, 'L0_tok_W_dt': 39.369, 'L0_attn_Wqkv': 3.926}
    for name, (base, spread) in spreads.items():
        noise = np.random.default_rng([zlib.crc32(name.encode()), seed]).standard_normal(out[name].shape)
        drawn = base * np.exp(spread * noise) if base else spread * noise
        out[name] = jnp.asarray(drawn.astype(out[name].dtype))
    for name, factor in factors.items():
        out[name] = (out[name] * factor).astype(out[name].dtype)
    return out
```

```python
from contextlib import ExitStack

import concourse.bass as bass
from concourse import mybir

ALU = mybir.AluOpType
ACT = mybir.ActivationFunctionType
F32 = mybir.dt.float32
I32 = mybir.dt.int32
AX_X = mybir.AxisListType.X

P = 128
UNDERFLOW = -87.5
CLAMP = 40.0
LN_EPS = 1e-5
NORM_EPS = 1e-12
LN2 = 0.6931471805599453


def audio_tower(nc, x, A_log, Dp, W_dbc, W_dt, b_dt, Wqkv, bqkv, Wproj, bproj, temperature,
                r_w1, r_b1, r_w2, r_b2, e_w1, e_b1, e_w2, e_b2, e_w3, e_b3, out):
    NBATCH, _, E = x.shape
    LAYERS, _, NS = A_log.shape
    H = temperature.shape[1]
    HD = E // H
    NX, _, HID = e_w1.shape
    RH = r_w1.shape[1]
    TOUT = out.shape[1]
    T = [TOUT << (LAYERS - 1 - l) for l in range(LAYERS)]
    GB = 8
    NPAIR = GB // 2
    NG = NBATCH // GB
    COLS = 4 * TOUT
    UNITS = [2, 1, 1]
    NBANK = [2, 2, 1]
    XJ = 3
    XP = T[0] // XJ
    NEP = NX // 2
    SCALE2 = float(HD) ** 0.5
    assert 2 * E == P and NS == 64 and COLS <= 512 and XP <= P and LAYERS == 3

    ctx = ExitStack()
    with ctx:
        def sb(name, shape, dt=F32):
            return ctx.enter_context(nc.sbuf_tensor(name, shape, dt))

        sems = {}

        def sem(name):
            if name not in sems:
                sems[name] = ctx.enter_context(nc.semaphore(name))
            return sems[name]

        NSLOT = 4
        ring = ctx.enter_context(nc.psum_tensor("ring", [P, NSLOT, 2, 512], F32))

        ident = sb("ident", [P, P])
        blk = sb("blk", [P, P])
        blk_half = sb("blk_half", [P, P])
        blk_mean = sb("blk_mean", [P, P])
        blk_head = sb("blk_head", [P, P])
        four = sb("four", [TOUT, TOUT])
        zero_col = sb("zero_col", [P, 1])
        clamp_col = sb("clamp_col", [P, 1])
        under_col = sb("under_col", [P, 1])
        two_col = sb("two_col", [P, 1])
        ln_col = sb("ln_col", [P, 1])
        eps_col = sb("eps_col", [P, 1])
        rank = sb("rank", [TOUT, GB, NX])
        w_bc = sb("w_bc", [P, LAYERS, 2, E])
        w_c0 = sb("w_c0", [NS, LAYERS, 2, E])
        w_d = sb("w_d", [1, LAYERS, 2, E])
        w_t = sb("w_t", [1, LAYERS, 2, E])
        wT = sb("wT", [P, LAYERS, 2 * NS])
        m_quad = sb("m_quad", [P, LAYERS, P])
        m_delta = sb("m_delta", [P, LAYERS, P])
        m_b0 = sb("m_b0", [P, LAYERS, P])
        m_c0 = sb("m_c0", [P, LAYERS, P])
        decay = sb("decay", [P, LAYERS, NS])
        decay_max = sb("decay_max", [P, LAYERS])
        d_col = sb("d_col", [P, LAYERS])
        bdt_col = sb("bdt_col", [P, LAYERS])
        nbdt_col = sb("nbdt_col", [P, LAYERS])
        wqkv_in = sb("wqkv_in", [P, 2, E])
        wv_in = sb("wv_in", [E, 2, E])
        wp_in = sb("wp_in", [E, 2, E])
        wq_bd = sb("wq_bd", [P, P])
        wk_bd = sb("wk_bd", [P, P])
        wv_bd = sb("wv_bd", [P, P])
        wp_bd = sb("wp_bd", [P, P])
        bqk_col = sb("bqk_col", [P, 2])
        bv_row = sb("bv_row", [TOUT, 2, E])
        bp_col = sb("bp_col", [P, 1])
        temp_col = sb("temp_col", [P, 1])
        head16 = sb("head16", [P, 16])
        mask_q = sb("mask_q", [P, 4])
        rw1 = sb("rw1", [P, 2 * RH])
        rb1_col = sb("rb1_col", [2 * RH, 1])
        rw2 = sb("rw2", [2 * RH, 2, NX])
        rb2_row = sb("rb2_row", [TOUT, NX])
        w1 = sb("w1", [P, NX, HID])
        w2 = sb("w2", [P, NEP, P])
        w3 = sb("w3", [P, NEP, E])
        b1_col = sb("b1_col", [P, NEP])
        b2_col = sb("b2_col", [P, NEP])
        b3 = sb("b3", [2 * NX, 2, E])
        sel = sb("sel", [2 * NX, 2, NEP, P])

        def per_unit(name, l, extra=0):
            return [sb(f"{name}{l}_{u}", [P, NBANK[l] * COLS + extra]) for u in range(UNITS[l])]

        xin = [sb(f"xin{u}", [XP, 2, XJ, 2, E]) for u in range(2)]
        xs = [per_unit("x", l) for l in range(LAYERS)]
        soft = [per_unit("soft", l) for l in range(LAYERS)]
        delta = [per_unit("delta", l) for l in range(LAYERS)]
        du = [per_unit("du", l) for l in range(LAYERS)]
        dec = [per_unit("dec", l) for l in range(LAYERS)]
        vin = [per_unit("vin", l, 1) for l in range(LAYERS)]
        carry = [per_unit("carry", l) for l in range(LAYERS)]
        base = [per_unit("base", l) for l in range(LAYERS)]
        flag_new = sb("flag_new", [P, 4])
        flags = sb("flags", [P, 4])
        gen_w = sb("gen_w", [P, 2, P])
        gen_a = sb("gen_a", [P, 1])

        h_in = sb("h_in", [P, COLS])
        h_mid = sb("h_mid", [P, COLS])
        cen = {s: sb(f"cen_{s}", [P, COLS]) for s in "af"}
        nrm = {s: sb(f"nrm_{s}", [P, COLS]) for s in "af"}
        rstd = {s: sb(f"rstd_{s}", [P, COLS]) for s in "af"}
        qk = sb("qk", [P, 2, COLS])
        qk_sq = sb("qk_sq", [P, 2, COLS])
        q_exp = sb("q_exp", [P, NPAIR, 4, TOUT])
        v1 = sb("v1", [TOUT, NPAIR, 2 * H, HD + 1])
        pm = [[sb(f"pm{b}{h}", [TOUT, 2, 4, TOUT]) for h in range(2)] for b in range(2)]
        y_rec = sb("y_rec", [TOUT, NPAIR, 2 * H])
        att = sb("att", [TOUT, NPAIR, 2 * H, HD])
        attT = sb("attT", [P, COLS])
        rh = sb("rh", [2 * RH, COLS])
        lg = sb("lg", [TOUT, GB, NX])
        pr = sb("pr", [TOUT, GB, NX])
        key = sb("key", [TOUT, GB, NX])
        oh = [sb(f"oh{k}", [TOUT, GB, NX]) for k in range(2)]
        st = sb("st", [TOUT, 8, GB])
        gate = sb("gate", [TOUT, GB, NX])
        gateT = sb("gateT", [2 * NX, COLS])
        hid1 = sb("hid1", [P, 2, COLS])
        hid2 = sb("hid2", [P, 2, COLS])
        hidw = [sb(f"hidw{k}", [P, 2, COLS]) for k in range(NEP)]
        osb = sb("osb", [TOUT, GB, E])
        flag_f = sb("flag_f", [1, 1])
        flag_sum = sb("flag_sum", [P, 1])
        flag_i = sb("flag_i", [1, 1], I32)

        STAGES = [("ffn", 4), ("att", 3), ("L2", 2), ("L1", 1), ("L0u0", 0), ("L0u1", 0)]
        BEHIND = dict(STAGES)
        DEPTH = max(BEHIND.values())
        LASTP = 12
        SSM_JOBS = {1: [("dpre", "dve delta")], 2: [("z", "dve quad")], 3: [("b", "dve vin")],
                    4: [("s", "dve base")], 5: [("c", "dve carry")]}
        L0_JOBS = {0: [("xT", "act x")], **SSM_JOBS}
        JOBS = {
            "L0u0": L0_JOBS, "L0u1": L0_JOBS, "L1": SSM_JOBS, "L2": SSM_JOBS,
            "att": {0: [("mean", "dve cen")], 1: [("var", "act ln")], 2: [("qk", "dve k")], 3: [("n2", "dve rk")],
                    4: [("v", "dve v1")], 5: [("s00", "act pm00"), ("s01", "act pm01")],
                    6: [("s10", "act pm10"), ("s11", "act pm11"), ("y0", "dve att0")],
                    7: [("s20", "act pm20"), ("s21", "act pm21"), ("y1", "dve att1")],
                    8: [("s30", "act pm30"), ("s31", "act pm31"), ("y2", "dve att2")],
                    9: [("y3", "dve att3")], 10: [("aT", "act attT")], LASTP: [("proj", "dve mid")]},
            "ffn": {0: [("mean", "dve cen")], 1: [("var", "act ln")], 2: [("rh", "act rh")], 3: [("lg", "dve lg")],
                    4: [("gT", "act gateT")], 5: [("h1_0", "act hid1_0")],
                    6: [("h2_0", "act hid2_0"), ("g_0", "dve hidw0"), ("h1_1", "act hid1_1")],
                    7: [("h2_1", "act hid2_1"), ("g_1", "dve hidw1"), ("h1_2", "act hid1_2")],
                    8: [("h2_2", "act hid2_2"), ("g_2", "dve hidw2")], 9: [("o", "act out")]},
        }
        SSM_ACT = ["relu", "exp", "ln", "alive", "decay"]
        SSM_DVE = ["delta", "quad", "vin", "scan", "base", "based", "carry"]
        SSM_POOL = ["du", "flag", "y", "pooled"]
        STEPS = {f"pe {s}": [j for ph in sorted(JOBS[s]) for j, _ in JOBS[s][ph]] for s, _ in STAGES}
        for s_ in ("L0u0", "L0u1", "L1", "L2"):
            STEPS[f"act {s_}"] = (["x"] if s_[:2] == "L0" else []) + SSM_ACT
            STEPS[f"dve {s_}"] = SSM_DVE
            STEPS[f"pool {s_}"] = SSM_POOL[:3] if s_ == "L2" else SSM_POOL
        STEPS["act att"] = ["sq", "ln", "rstd", "qksq", "lnorm", "rnorm"] + [f"pm{q}{h}" for q in range(4) for h in range(2)] + ["attT"]
        STEPS["dve att"] = ["cen", "hn", "q", "k", "rq", "rk", "hat", "v1"] + \
            [f"{w}{q}" for q in range(4) for w in ("rec", "att")] + ["mid"]
        STEPS["pool att"] = ["qe"]
        STEPS["act ffn"] = ["sq", "ln", "rstd", "rh", "prexp", "topexp", "gateT", "hid1_0", "hid2_0", "hid1_1",
                            "hid2_1", "hid1_2", "hid2_2", "out"]
        ROUTE1 = ["lg", "mx", "shift", "sum", "rsum", "pr"]
        TOP = ["m", "eq", "key", "kmax", "oh"]
        ROUTE2 = [f"{w}0" for w in TOP] + ["rest"] + [f"{w}1" for w in TOP] + ["diff", "den", "r0", "r1", "g0", "g1", "gate"]
        STEPS["dve ffn"] = ["cen", "hn"] + ROUTE1 + ROUTE2 + ["hidw0", "hidw1", "hidw2"]
        STEPS["sp L0u0"] = STEPS["sp L0u1"] = [f"load{b}" for b in range(4)]
        STEPS["sp ffn"] = ["store"]
        done = {who: sem(who.replace(" ", "_")) for who in STEPS}

        OVERLAPPED = [(s, ph) for ph in range(LASTP + 1) for s, _ in STAGES]
        IN_ORDER = [(s, ph) for s in ("L0u0", "L0u1", "L1", "L2", "att", "ffn") for ph in range(LASTP + 1)]

        def slots_of(order):
            jobs = [(s, j, r) for s, ph in order for j, r in JOBS[s].get(ph, ())]
            last, slots = {}, {}
            for again in (0, 1):
                for at, (s, j, r) in enumerate(jobs):
                    k = at % NSLOT
                    earlier = last.get(k)
                    slots[s, j] = (k, earlier and (*earlier[:2], earlier[2] < again))
                    last[k] = (s, r, again)
            return slots, jobs

        class Turn:

            def __init__(self, order, first, k, overlapped):
                self.first, self.k, self.overlapped = first, k, overlapped
                self.live = [s for s, b in STAGES if not overlapped or not isinstance(first, int)
                             or 0 <= first - b < NG]
                self.order = [(s, ph) for s, ph in order if s in self.live]
                self.slots, self.jobs = slots_of(order)

            def group(self, s):
                return self.k + (self.first - BEHIND[s]) if self.overlapped else self.k + NG

            def batch(self, s):
                return self.group(s) if self.overlapped else self.k

            def slot(self, s, job):
                return self.slots[s, job][0]

        def need(eng, t, who, step, group=None, back=0):
            g = (t.group(who.split()[1]) if group is None else group) - back
            steps = STEPS[who]
            by = 16 if who[:2] == "sp" else 1
            if isinstance(g, int):
                if g < 0:
                    return
            eng.wait_ge(done[who], g * (by * len(steps)) + by * (steps.index(step) + 1))

        def slot_for(eng, t, s, job):
            k, earlier = t.slots[s, job]
            es, er, turn_before = earlier
            if isinstance(t.group(es), int):
                at = [(a, b) for a, b, _ in t.jobs].index((s, job))
                for i in range(at - 1, at - 4 * len(t.jobs), -1):
                    a, _, r = t.jobs[i % len(t.jobs)]
                    g = t.group(a) + i // len(t.jobs)
                    if i % len(t.jobs) % NSLOT == k and 0 <= g < NG:
                        need(eng, t, f"{r.split()[0]} {a}", r.split()[1], group=g)
                        break
            else:
                need(eng, t, f"{er.split()[0]} {es}", er.split()[1], group=t.group(es) - turn_before)
            return ring[:, k]

        def walk(eng, do):
            def turn(t):
                for s, ph in t.order:
                    do(t, s, ph)
            for i in range(DEPTH + 1):
                turn(Turn(OVERLAPPED, i, 0, True))
            with eng.Fori(0, NG - DEPTH - 1) as k:
                t = Turn(OVERLAPPED, DEPTH + 1, k, True)
                turn(t)
            for i in range(NG, NG + DEPTH):
                turn(Turn(OVERLAPPED, i, 0, True))

        def walk_general(eng, do):
            with eng.Fori(0, NG) as k:
                t = Turn(IN_ORDER, 0, k, False)
                for s, ph in t.order:
                    do(t, s, ph)

        def layer_unit(s):
            return int(s[1]), int(s[3]) if len(s) > 2 else 0

        def banks(ap, n):
            return ap.rearrange("p (b c) -> p b c", b=n)

        NPREP = 77
        prep = {n: sem(f"prep_{n}") for n in ("dma", "pe", "copy", "const", "done", "exp", "flag")}
        blocks4 = [(l, k) for l in range(LAYERS) for k in range(2)]

        block = ctx.enter_context(nc.Block())

        @block.sync
        def _(sp):
            n = [0]

            def load(dst, src):
                sp.dma_start(dst, src, allow_slow_non_contiguous=True).then_inc(prep["dma"], 16)
                n[0] += 1

            def load_x(s, first):
                _, u = layer_unit(s)
                for b in range(4):
                    sp.dma_start(xin[u][:, b // 2, :, b % 2, :],
                                 x[bass.ds(first + u * 4 + b, 1), 0:T[0], :].rearrange(
                                     "b (p j) e -> p (b j) e", j=XJ)).then_inc(done[f"sp {s}"], 16)

            for l in range(LAYERS):
                for k in range(2):
                    load(w_bc[:, l, k, :], W_dbc[l, 1:1 + 2 * NS, :])
                    load(w_c0[:, l, k, :], W_dbc[l, 1 + NS:1 + 2 * NS, :])
                    load(w_d[:, l, k, :], W_dbc[l, 0:1, :])
                    load(w_t[:, l, k, :], W_dt[l, :, :].rearrange("e r -> r e"))
            load_x("L0u0", 0)
            load_x("L0u1", 0)
            for k in range(2):
                half = slice(E * k, E * k + E)
                load(decay[half, :, :], A_log.rearrange("l e n -> e l n"))
                load(d_col[half, :], Dp.rearrange("l e -> e l"))
                load(bdt_col[half, :], b_dt.rearrange("l e -> e l"))
                load(wqkv_in[:, k, :], Wqkv[0:P, :])
                load(wv_in[:, k, :], Wqkv[P:P + E, :])
                load(wp_in[:, k, :], Wproj)
                load(bqk_col[half, :], bqkv[0:P].rearrange("(c e) -> e c", c=2))
                load(bv_row[:, k, :], bqkv[P:P + E].rearrange("(a e) -> a e", a=1).broadcast_to([TOUT, E]))
                load(bp_col[half, :], bproj.rearrange("(e a) -> e a", a=1))
                for h in range(H):
                    load(temp_col[E * k + HD * h:E * k + HD * h + HD, :],
                         temperature[0, h:h + 1, :, 0].broadcast_to([HD, 1]))
                load(rb1_col[RH * k:RH * k + RH, :], r_b1.rearrange("(e a) -> e a", a=1))
                load(w1[half, :, :], e_w1.rearrange("x d h -> d x h"))
                load(w3[half, :, :], e_w3.rearrange("(c k) h o -> k h c o", k=2)[k])
                load(b1_col[half, :], e_b1.rearrange("(c k) h -> k h c", k=2)[k])
                load(b2_col[half, :], e_b2.rearrange("(c k) h -> k h c", k=2)[k])
            load(rb2_row[:], r_b2.rearrange("(a e) -> a e", a=1).broadcast_to([TOUT, NX]))
            sp.wait_ge(prep["const"], 4)
            for k in range(2):
                half = slice(E * k, E * k + E)
                load(rw1[half, RH * k:RH * k + RH], r_w1)
                load(rw2[RH * k:RH * k + RH, k, :], r_w2)
                load(w2[half, :, half], e_w2.rearrange("(c k) h f -> k h c f", k=2)[k])
                load(b3[NX * k:NX * k + NX, k, :], e_b3)
            assert n[0] == NPREP

            def do(t, s, ph):
                if s[:2] == "L0" and ph == 0:
                    g = t.group(s)
                    if isinstance(g, int) and g == 0:
                        return
                    need(sp, t, f"pe {s}", "xT", back=1)
                    load_x(s, t.batch(s) * GB)
                if s == "ffn" and ph == 10:
                    need(sp, t, "act ffn", "out")
                    sp.dma_start(out[bass.ds(t.batch(s) * GB, GB), :, :].rearrange("b t e -> t b e"),
                                 osb[:]).then_inc(done["sp ffn"], 16)

            walk(sp, do)
            sp.wait_ge(done["sp ffn"], 16 * NG)
            sp.wait_ge(prep["flag"], 1)
            again = sp.value_load(flag_i[0:1, 0:1], min_val=0, max_val=1)
            with sp.If(again != 0):
                walk_general(sp, do)
                sp.wait_ge(done["sp ffn"], 32 * NG)

        @block.gpsimd
        def _(pool):
            g = nc.gpsimd
            cst = sem("masks")
            g.memset(ident[:], 0.0).then_inc(cst, 1)
            g.memset(sel[:], 0.0).then_inc(cst, 1)
            g.memset(blk_head[:], 1.0).then_inc(cst, 1)
            g.memset(head16[:], 1.0).then_inc(cst, 1)
            pool.wait_ge(cst, 4)
            g.affine_select(out=ident[:], in_=ident[:], compare_op=ALU.not_equal, fill=1.0, base=0,
                            pattern=[[-1, P]], channel_multiplier=1).then_inc(cst, 1)
            sv = sel[:].rearrange("r a b (x m) -> r (a b x) m", x=2)
            g.affine_select(out=sv, in_=sv, compare_op=ALU.not_equal, fill=1.0, base=0,
                            pattern=[[-1, 2 * NX], [0, HID]], channel_multiplier=1).then_inc(cst, 1)
            for off, mult in ((0, 1), (HD - 1, -1)):
                for t_, c in ((blk_head, HD), (head16, 1)):
                    v = t_[:].rearrange("p (a c) -> p a c", c=c)
                    g.affine_select(out=v, in_=v, compare_op=ALU.is_ge, fill=0.0, base=off,
                                    pattern=[[-HD * mult, P // HD], [0, c]],
                                    channel_multiplier=mult).then_inc(cst, 1)
                pool.wait_ge(cst, 8 if mult == 1 else 10)
            g.memset(flags[:], 0.0).then_inc(cst, 1)
            pool.wait_ge(cst, 11)
            pool.wait_ge(prep["done"], 1)

            def ssm(t, s, ph):
                l, u = layer_unit(s)
                me = done[f"pool {s}"]
                f = u if l == 0 else l + 1
                if ph == 1:
                    need(pool, t, f"dve {s}", "delta")
                    g.tensor_tensor(du[l][u][:], delta[l][u][:], xs[l][u][:], ALU.mult).then_inc(me, 1)
                if ph == 2:
                    need(pool, t, f"act {s}", "alive")
                    need(pool, t, f"pool {s}", "flag", back=1)
                    g.tensor_tensor(flags[:, f:f + 1], flags[:, f:f + 1], flag_new[:, f:f + 1],
                                    ALU.add).then_inc(me, 1)
                if ph == LASTP:
                    need(pool, t, f"dve {s}", "carry")
                    if l == LAYERS - 1:
                        need(pool, t, "dve att", "mid", group=t.group(s) - 1)
                        g.tensor_tensor(h_in[:], base[l][u][:], carry[l][u][:], ALU.add).then_inc(me, 1)
                        return
                    g.tensor_tensor(base[l][u][:], base[l][u][:], carry[l][u][:], ALU.add).then_inc(me, 1)
                    need(pool, t, f"pool {s}", "y")
                    need(pool, t, f"dve L{l + 1}", "carry", group=t.group(s) - 1)
                    pairs = base[l][u][:].rearrange("p (t two) -> p t two", two=2)
                    half = NBANK[l] * COLS // 2
                    g.tensor_tensor(xs[l + 1][0][:, u * half:(u + 1) * half], pairs[:, :, 0], pairs[:, :, 1],
                                    ALU.add).then_inc(me, 1)

            def do(t, s, ph):
                if s[0] == "L":
                    ssm(t, s, ph)
                if s == "att" and ph == 3:
                    need(pool, t, "dve att", "hat")
                    need(pool, t, "pe att", "s31", back=1)
                    wide = [P, NPAIR, 4, TOUT]
                    g.tensor_tensor(q_exp[:],
                                    qk[:, 0, :].rearrange("p (q t) -> p q t", q=NPAIR)[:, :, None, :].broadcast_to(wide),
                                    mask_q[:, None, :, None].broadcast_to(wide), ALU.mult).then_inc(done["pool att"], 1)

            walk(pool, do)
            pool.wait_ge(prep["flag"], 1)
            again = pool.value_load(flag_i[0:1, 0:1], min_val=0, max_val=1)
            with pool.If(again != 0):
                walk_general(pool, do)

        @block.scalar
        def _(act):
            a = nc.scalar
            act.wait_ge(prep["dma"], 16 * NPREP)
            a.activation(decay[:], decay[:], ACT.Exp).then_inc(prep["exp"], 1)
            act.wait_ge(prep["done"], 1)

            def ssm(t, s, ph):
                l, u = layer_unit(s)
                nb = NBANK[l]
                me = done[f"act {s}"]
                buf = soft[l][u][:]
                f = u if l == 0 else l + 1
                if ph == 0 and l == 0:
                    need(act, t, f"pe {s}", "xT")
                    need(act, t, f"dve {s}", "carry", back=1)
                    a.activation(banks(xs[0][u][:], nb), ring[:, t.slot(s, "xT"), 0:nb, 0:COLS],
                                 ACT.Copy).then_inc(me, 1)
                if ph == 1:
                    need(act, t, f"pe {s}", "dpre")
                    need(act, t, f"dve {s}", "carry", back=1)
                    a.activation(banks(buf, nb), ring[:, t.slot(s, "dpre"), 0:nb, 0:COLS], ACT.Relu,
                                 bias=nbdt_col[:, l:l + 1], scale=-1.0).then_inc(me, 1)
                    need(act, t, f"act {s}", "relu")
                    a.activation(buf, buf, ACT.Exp, bias=clamp_col[:], scale=-1.0).then_inc(me, 1)
                    need(act, t, f"act {s}", "exp")
                    a.activation(buf, buf, ACT.Ln, bias=1.0).then_inc(me, 1)
                if ph == 2:
                    need(act, t, f"dve {s}", "delta")
                    need(act, t, f"pool {s}", "flag", back=1)
                    dl = delta[l][u][:].rearrange("p (q t) -> p q t", t=T[l])[:, :, 1:]
                    dc = dec[l][u][:].rearrange("p (q t) -> p q t", t=T[l])[:, :, 1:]
                    a.activation(dc, dl, ACT.Relu, bias=under_col[:], scale=decay_max[:, l:l + 1],
                                 accum_out=flag_new[:, f:f + 1]).then_inc(me, 1)
                    need(act, t, f"act {s}", "alive")
                    a.activation(dc, dl, ACT.Exp, scale=decay[:, l, 0:1]).then_inc(me, 1)

            def norm(t, s, ph):
                w, me = s[0], done[f"act {s}"]
                if ph == 0:
                    need(act, t, f"dve {s}", "cen")
                    a.activation(rstd[w][:], cen[w][:], ACT.Square).then_inc(me, 1)
                if ph == 1:
                    need(act, t, f"pe {s}", "var")
                    a.activation(rstd[w][:], ring[:, t.slot(s, "var"), 0, 0:COLS], ACT.Ln,
                                 bias=eps_col[:]).then_inc(me, 1)
                    need(act, t, f"act {s}", "ln")
                    a.activation(rstd[w][:], rstd[w][:], ACT.Exp, scale=-0.5).then_inc(me, 1)

            def attention(t, s, ph):
                norm(t, s, ph)
                me = done["act att"]
                if ph == 2:
                    need(act, t, "dve att", "k")
                    a.activation(qk_sq[:], qk[:], ACT.Square).then_inc(me, 1)
                if ph == 3:
                    need(act, t, "dve att", "rk")
                    a.activation(qk_sq[:], qk_sq[:], ACT.Ln, scale=2.0 ** 24).then_inc(me, 1)
                    need(act, t, "act att", "lnorm")
                    a.activation(qk_sq[:], qk_sq[:], ACT.Exp, bias=ln_col[:], scale=-0.5).then_inc(me, 1)
                if 5 <= ph <= 8:
                    q = ph - 5
                    for h in range(2):
                        need(act, t, "pe att", f"s{q}{h}")
                        need(act, t, "pe att", f"y{(q - 2) % 4}", back=1 if q < 2 else 0)
                        a.activation(pm[q % 2][h][:].rearrange("m a j n -> m a (j n)"),
                                     ring[0:TOUT, t.slot(s, f"s{q}{h}"), :, 0:COLS], ACT.Square,
                                     bias=two_col[0:TOUT], scale=0.5 ** 0.5).then_inc(me, 1)
                if ph == 10:
                    need(act, t, "pe att", "aT")
                    a.activation(attT[:], ring[:, t.slot(s, "aT"), 0, 0:COLS], ACT.Copy).then_inc(me, 1)

            def experts(t, s, ph):
                norm(t, s, ph)
                me = done["act ffn"]

                def relu(dst, job, bias, rows=P, nb=2):
                    need(act, t, "pe ffn", job)
                    k = t.slot(s, job)
                    src = ring[0:rows, k, :, 0:COLS] if nb == 2 else ring[0:rows, k, 0, 0:COLS]
                    a.activation(dst[:], src, ACT.Relu, bias=bias).then_inc(me, 1)

                if ph == 2:
                    relu(rh, "rh", rb1_col[:], rows=2 * RH, nb=1)
                if ph == 3:
                    need(act, t, "dve ffn", "shift")
                    a.activation(pr[:], lg[:], ACT.Exp).then_inc(me, 1)
                    need(act, t, "dve ffn", "diff")
                    a.activation(st[:, 6, :], st[:, 5, :], ACT.Exp).then_inc(me, 1)
                if ph == 4:
                    need(act, t, "pe ffn", "gT")
                    a.activation(gateT[:], ring[0:2 * NX, t.slot(s, "gT"), 0, 0:COLS], ACT.Copy).then_inc(me, 1)
                k = ph - 6
                if 0 <= k < NEP:
                    need(act, t, "dve ffn", f"hidw{(k - 1) % NEP}", back=0 if k else 1)
                    relu(hid2, f"h2_{k}", b2_col[:, k:k + 1])
                if 0 <= k + 1 < NEP:
                    relu(hid1, f"h1_{k + 1}", b1_col[:, k + 1:k + 2])
                if ph == 9:
                    need(act, t, "pe ffn", "o")
                    need(act, t, "sp ffn", "store", back=1)
                    a.activation(osb[:].rearrange("t b e -> t (b e)"), ring[0:TOUT, t.slot(s, "o"), 0, :],
                                 ACT.Copy).then_inc(me, 1)

            def do(t, s, ph):
                {"L": ssm, "a": attention, "f": experts}[s[0]](t, s, ph)

            def do_general(t, s, ph):
                do(t, s, ph)
                if s[0] == "L" and ph == 5:
                    l, u = layer_unit(s)
                    dl = delta[l][u][:].rearrange("p (q t) -> p q t", t=T[l])[:, :, 1:]
                    dc = dec[l][u][:].rearrange("p (q t) -> p q t", t=T[l])[:, :, 1:]
                    done_before = t.k * (4 * (NS - 1)) + (l + u + (1 if l else 0)) * (NS - 1)
                    with act.Fori(1, NS) as n:
                        act.wait_ge(sem("gen_weights"), done_before + n)
                        a.activation(dc, dl, ACT.Exp, scale=gen_a[:]).then_inc(sem("gen_decay"), 1)

            walk(act, do)
            act.wait_ge(prep["flag"], 1)
            again = act.value_load(flag_i[0:1, 0:1], min_val=0, max_val=1)
            with act.If(again != 0):
                walk_general(act, do_general)

        @block.tensor
        def _(pe):
            mm = nc.tensor.matmul

            pe.wait_ge(prep["dma"], 16 * NPREP)
            pe.wait_ge(sem("masks"), 11)
            for l in range(LAYERS):
                o = ring[:, l, 0]
                two = "r k e -> r (k e)"
                mm(o[:, 0:P], w_bc[0:NS, l].rearrange(two), w_c0[:, l].rearrange(two), start=True, stop=True)
                mm(o[:, P:2 * P], w_d[:, l].rearrange(two), w_t[:, l].rearrange(two), start=True, stop=True)
                nc.tensor.transpose(o[:, 2 * P:3 * P], w_bc[:, l].rearrange(two), ident[:]).then_inc(prep["pe"], 1)
            o = ring[:, 3, 0]
            nc.tensor.transpose(o[:, 0:P], wqkv_in[:].rearrange("r k e -> r (k e)"), ident[:])
            nc.tensor.transpose(o[:, P:P + E], wv_in[:].rearrange("r k e -> r (k e)"), ident[0:E, 0:E])
            nc.tensor.transpose(o[:, P + E:2 * P], wp_in[:].rearrange("r k e -> r (k e)"),
                                ident[0:E, 0:E]).then_inc(prep["pe"], 1)
            pe.wait_ge(prep["done"], 1)

            def ssm(t, s, ph):
                l, u = layer_unit(s)
                nb = NBANK[l]
                me = done[f"pe {s}"]
                if ph == 0 and l == 0:
                    need(pe, t, f"sp {s}", "load3")
                    o = slot_for(pe, t, s, "xT")
                    for q in range(2):
                        for j in range(XJ):
                            ins = nc.tensor.transpose(
                                o[:, q, 0:COLS].rearrange("p (t j) -> p t j", j=XJ)[:, :, j],
                                xin[u][:, q, j].rearrange("p h e -> p (h e)"), ident[0:XP, 0:XP])
                    ins.then_inc(me, 1)
                    return
                if ph not in SSM_JOBS:
                    return
                job = SSM_JOBS[ph][0][0]
                if job == "s":
                    need(pe, t, f"dve {s}", "quad")
                    w, src = (blk_half if l < LAYERS - 1 else blk)[:], soft[l][u]
                else:
                    w = {"dpre": m_delta, "z": m_quad, "b": m_b0, "c": m_c0}[job][:, l]
                    src = xs[l][u]
                    if l == 0:
                        need(pe, t, f"act {s}", "x")
                    elif l == 1:
                        need(pe, t, "pool L0u0", "pooled", group=t.group(s))
                        need(pe, t, "pool L0u1", "pooled", group=t.group(s))
                    else:
                        need(pe, t, "pool L1", "pooled", group=t.group(s))
                o = slot_for(pe, t, s, job)
                for b in range(nb):
                    ins = mm(o[:, b, 0:COLS], w, src[:, b * COLS:(b + 1) * COLS], start=True, stop=True)
                ins.then_inc(me, 1)

            def norm(t, s, ph, h):
                me = done[f"pe {s}"]
                if ph == 0:
                    o = slot_for(pe, t, s, "mean")
                    mm(o[:, 0, 0:COLS], blk_mean[:], h[:], start=True, stop=True).then_inc(me, 1)
                if ph == 1:
                    need(pe, t, f"act {s}", "sq")
                    o = slot_for(pe, t, s, "var")
                    mm(o[:, 0, 0:COLS], blk_mean[:], rstd[s[0]][:], start=True, stop=True).then_inc(me, 1)

            def attention(t, s, ph):
                me = done["pe att"]
                hn = nrm["a"]
                if ph == 0:
                    need(pe, t, "pool L2", "y", group=t.group(s))
                norm(t, s, ph, h_in)
                if ph == 2:
                    need(pe, t, "dve att", "hn")
                    o = slot_for(pe, t, s, "qk")
                    mm(o[:, 0, 0:COLS], wq_bd[:], hn[:], start=True, stop=True)
                    mm(o[:, 1, 0:COLS], wk_bd[:], hn[:], start=True, stop=True).then_inc(me, 1)
                if ph == 3:
                    need(pe, t, "act att", "qksq")
                    o = slot_for(pe, t, s, "n2")
                    for b in range(2):
                        ins = mm(o[:, b, 0:COLS], blk_head[:], qk_sq[:, b, :], start=True, stop=True)
                    ins.then_inc(me, 1)
                if ph == 4:
                    o = slot_for(pe, t, s, "v")
                    for q in range(NPAIR):
                        ins = mm(o[0:TOUT, 0, q * P:(q + 1) * P], hn[:, q * TOUT:(q + 1) * TOUT], wv_bd[:],
                                 start=True, stop=True)
                    ins.then_inc(me, 1)
                if 5 <= ph <= 8:
                    q = ph - 5
                    need(pe, t, "pool att", "qe")
                    for h in range(2):
                        o = slot_for(pe, t, s, f"s{q}{h}")
                        for b in range(2):
                            r = E * h + 32 * b
                            ins = mm(o[0:TOUT, b, 0:COLS], qk[r:r + 32, 1, q * TOUT:(q + 1) * TOUT],
                                     q_exp[r:r + 32, q].rearrange("p j n -> p (j n)"), start=True, stop=True,
                                     tile_position=(r, 0))
                        ins.then_inc(me, 1)
                if 6 <= ph <= 9:
                    q = ph - 6
                    need(pe, t, "dve att", "v1")
                    need(pe, t, "act att", f"pm{q}1")
                    o = slot_for(pe, t, s, f"y{q}")
                    w = HD + 1
                    mm(o[0:TOUT, 0, 0:2 * H * w], four[:], v1[:, q].rearrange("m h d -> m (h d)"),
                       start=True, stop=False, skip_group_check=True)
                    for hh in range(2 * H):
                        h, b, j = hh // H, hh % H // 4, hh % 4
                        ins = mm(o[0:TOUT, 0, hh * w:(hh + 1) * w], pm[q % 2][h][:, b, j, :], v1[:, q, hh, :],
                                 start=False, stop=(hh == 2 * H - 1), skip_group_check=True)
                    ins.then_inc(me, 1)
                if ph == 10:
                    need(pe, t, "dve att", "att3")
                    o = slot_for(pe, t, s, "aT")
                    for q in range(NPAIR):
                        ins = nc.tensor.transpose(o[:, 0, q * TOUT:(q + 1) * TOUT],
                                                  att[:, q].rearrange("m h d -> m (h d)"), ident[0:TOUT, 0:TOUT])
                    ins.then_inc(me, 1)
                if ph == LASTP:
                    need(pe, t, "act att", "attT")
                    o = slot_for(pe, t, s, "proj")
                    mm(o[:, 0, 0:COLS], wp_bd[:], attT[:], start=True, stop=True).then_inc(me, 1)

            def experts(t, s, ph):
                me = done["pe ffn"]
                hn = nrm["f"]
                if ph == 0:
                    need(pe, t, "dve att", "mid", group=t.group(s))
                norm(t, s, ph, h_mid)
                if ph == 2:
                    need(pe, t, "dve ffn", "hn")
                    o = slot_for(pe, t, s, "rh")
                    mm(o[0:2 * RH, 0, 0:COLS], rw1[:], hn[:], start=True, stop=True).then_inc(me, 1)
                if ph == 3:
                    need(pe, t, "act ffn", "rh")
                    o = slot_for(pe, t, s, "lg")
                    for q in range(NPAIR):
                        ins = mm(o[0:TOUT, 0, q * 2 * NX:(q + 1) * 2 * NX], rh[:, q * TOUT:(q + 1) * TOUT],
                                 rw2[:].rearrange("r k e -> r (k e)"), start=True, stop=True)
                    ins.then_inc(me, 1)
                if ph == 4:
                    need(pe, t, "dve ffn", "gate")
                    o = slot_for(pe, t, s, "gT")
                    for q in range(NPAIR):
                        ins = nc.tensor.transpose(o[0:2 * NX, 0, q * TOUT:(q + 1) * TOUT],
                                                  gate[:, 2 * q:2 * q + 2, :].rearrange("m h e -> m (h e)"),
                                                  ident[0:TOUT, 0:TOUT])
                    ins.then_inc(me, 1)
                k = ph - 6
                if 0 <= k < NEP:
                    need(pe, t, "act ffn", f"hid1_{k}")
                    o = slot_for(pe, t, s, f"h2_{k}")
                    for h in range(2):
                        ins = mm(o[:, h, 0:COLS], w2[:, k], hid1[:, h], start=True, stop=True)
                    ins.then_inc(me, 1)
                    need(pe, t, "act ffn", "gateT")
                    o = slot_for(pe, t, s, f"g_{k}")
                    for h in range(2):
                        ins = mm(o[:, h, 0:COLS], sel[:, h, k], gateT[:], start=True, stop=True)
                    ins.then_inc(me, 1)
                if 0 <= k + 1 < NEP:
                    o = slot_for(pe, t, s, f"h1_{k + 1}")
                    for h in range(2):
                        ins = mm(o[:, h, 0:COLS], w1[E * h:E * h + E, 2 * k + 2:2 * k + 4].rearrange("p x m -> p (x m)"),
                                 hn[E * h:E * h + E, :], start=True, stop=True, tile_position=(E * h, 0))
                    ins.then_inc(me, 1)
                if ph == 9:
                    need(pe, t, "dve ffn", f"hidw{NEP - 1}")
                    o = slot_for(pe, t, s, "o")
                    for q in range(NPAIR):
                        cols = slice(q * TOUT, (q + 1) * TOUT)
                        for h in range(2):
                            dst = o[0:TOUT, 0, (2 * q + h) * E:(2 * q + h + 1) * E]
                            mm(dst, h_mid[:, cols], ident[:, E * h:E * h + E], start=True, stop=False)
                            for k in range(NEP):
                                mm(dst, hidw[k][:, h, cols], w3[:, k], start=False, stop=False)
                            ins = mm(dst, gateT[:, cols], b3[:, h], start=False, stop=True)
                    ins.then_inc(me, 1)

            def do(t, s, ph):
                {"L": ssm, "a": attention, "f": experts}[s[0]](t, s, ph)

            def do_general(t, s, ph):
                do(t, s, ph)
                if s[0] == "L" and ph == 5:
                    l, u = layer_unit(s)
                    ob, oc = ring[:, t.slot(s, "b")], ring[:, t.slot(s, "c")]
                    done_before = t.k * (4 * (NS - 1)) + (l + u + (1 if l else 0)) * (NS - 1)
                    with pe.Fori(1, NS) as n:
                        pe.wait_ge(sem("gen_weights"), done_before + n)
                        for o, k in ((ob, 0), (oc, 1)):
                            for b in range(NBANK[l]):
                                ins = mm(o[:, b, 0:COLS], gen_w[:, k], xs[l][u][:, b * COLS:(b + 1) * COLS],
                                         start=True, stop=True)
                        ins.then_inc(sem("gen_bc"), 1)
                    need(pe, t, f"dve {s}", "carry")

            walk(pe, do)
            pe.wait_ge(sem("flag_sum"), 1)
            need_all = done["act ffn"]
            pe.wait_ge(need_all, NG * len(STEPS["act ffn"]))
            mm(ring[0:1, 0, 0, 0:1], flag_sum[:], blk_mean[:, 0:1], start=True, stop=False, skip_group_check=True)
            mm(ring[0:1, 0, 0, 0:1], flag_sum[:], blk_mean[:, E:E + 1], start=False, stop=True,
               skip_group_check=True).then_inc(sem("flag_pe"), 1)
            pe.wait_ge(prep["flag"], 1)
            again = pe.value_load(flag_i[0:1, 0:1], min_val=0, max_val=1)
            with pe.If(again != 0):
                walk_general(pe, do_general)

        @block.vector
        def _(dve):
            v = nc.vector
            made = prep["const"]
            tt, ts, stt = v.tensor_tensor, v.tensor_scalar, v.scalar_tensor_tensor

            v.memset(rw1[:], 0.0).then_inc(made, 1)
            v.memset(rw2[:], 0.0).then_inc(made, 1)
            v.memset(w2[:], 0.0).then_inc(made, 1)
            v.memset(b3[:], 0.0).then_inc(made, 1)
            for t_, val in ((blk, 1.0), (blk_half, 0.5), (blk_mean, 1.0 / E)):
                v.memset(t_[:], 0.0).then_inc(made, 1)
            for t_ in (wq_bd, wk_bd, wv_bd, wp_bd):
                v.memset(t_[:], 0.0).then_inc(made, 1)
            dve.wait_ge(made, 11)
            for t_, val in ((blk, 1.0), (blk_half, 0.5), (blk_mean, 1.0 / E)):
                for k in range(2):
                    half = slice(E * k, E * k + E)
                    v.memset(t_[half, half], val).then_inc(made, 1)
            for t_, val in ((four, 4.0), (zero_col, 0.0), (clamp_col, CLAMP), (under_col, -UNDERFLOW),
                            (two_col, 2.0), (ln_col, 12.0 * LN2), (eps_col, LN_EPS), (v1, 1.0)):
                v.memset(t_[:], val).then_inc(made, 1)
            for e in range(NX):
                v.memset(rank[:, :, e:e + 1], float(NX - e)).then_inc(made, 1)
            cleared = [t_[u] for l in range(LAYERS) for t_ in (dec[l], vin[l]) for u in range(UNITS[l])]
            for t_ in cleared:
                v.memset(t_[:], 0.0).then_inc(made, 1)
            consts = 11 + 6 + 8 + NX + len(cleared)
            dve.wait_ge(made, consts)

            dve.wait_ge(prep["dma"], 16 * NPREP)
            dve.wait_ge(sem("masks"), 11)
            dve.wait_ge(prep["pe"], 4)
            dve.wait_ge(prep["exp"], 1)
            c = prep["copy"]
            n = 0
            for l in range(LAYERS):
                o = ring[:, l, 0]
                tt(m_quad[:, l], o[:, 0:P], blk[:], ALU.mult).then_inc(c, 1)
                tt(m_delta[:, l], o[:, P:2 * P], blk[:], ALU.mult).then_inc(c, 1)
                v.tensor_copy(wT[:, l], o[:, 2 * P:3 * P]).then_inc(c, 1)
                ts(decay[:, l], decay[:, l], -1.0, None, ALU.mult).then_inc(c, 1)
                ts(nbdt_col[:, l:l + 1], bdt_col[:, l:l + 1], -1.0, CLAMP, ALU.mult, ALU.add).then_inc(c, 1)
                n += 5
            for t_, at in ((wq_bd, 0), (wk_bd, E), (wv_bd, P), (wp_bd, P + E)):
                for k in range(2):
                    half = slice(E * k, E * k + E)
                    v.tensor_copy(t_[half, half], ring[half, 3, 0, at:at + E]).then_inc(c, 1)
                    n += 1
            v.tensor_reduce(mask_q[:], head16[:].rearrange("p (a j) -> p j a", j=4), AX_X, ALU.add).then_inc(c, 1)
            n += 1
            dve.wait_ge(c, n)
            for l in range(LAYERS):
                scale = 0.5 if l < LAYERS - 1 else 1.0
                ts(m_b0[:, l], blk[:], wT[:, l, 0:1], None, ALU.mult).then_inc(c, 1)
                ts(m_c0[:, l], blk[:], wT[:, l, NS:NS + 1], scale, ALU.mult, ALU.mult).then_inc(c, 1)
                v.tensor_reduce(decay_max[:, l:l + 1], decay[:, l, 1:NS], AX_X, ALU.max).then_inc(c, 1)
                ts(d_col[:, l:l + 1], d_col[:, l:l + 1], scale, None, ALU.mult).then_inc(c, 1)
                n += 4
            ts(mask_q[:], mask_q[:], temp_col[:, 0:1], SCALE2, ALU.mult, ALU.mult).then_inc(c, 1)
            dve.wait_ge(c, n + 1)
            v.memset(zero_col[:], 0.0).then_inc(prep["done"], 1)

            def ssm(t, s, ph, general=False):
                l, u = layer_unit(s)
                nb = NBANK[l]
                me = done[f"dve {s}"]
                X, W = banks(xs[l][u][:], nb), nb * COLS

                def made_by(job):
                    need(dve, t, f"pe {s}", job)
                    return ring[:, t.slot(s, job), 0:nb, 0:COLS]

                if ph == 1:
                    o = made_by("dpre")
                    need(dve, t, f"act {s}", "ln")
                    stt(banks(delta[l][u][:], nb), o, bdt_col[:, l:l + 1], banks(soft[l][u][:], nb),
                        ALU.add, ALU.max).then_inc(me, 1)
                if ph == 2:
                    o = made_by("z")
                    need(dve, t, f"dve {s}", "delta")
                    tt(banks(soft[l][u][:], nb), o, X, ALU.mult).then_inc(me, 1)
                if ph == 3:
                    o = made_by("b")
                    need(dve, t, f"pool {s}", "du")
                    tt(banks(vin[l][u][:, 1:W + 1], nb), o, banks(du[l][u][:], nb), ALU.mult).then_inc(me, 1)
                    need(dve, t, f"dve {s}", "vin")
                    need(dve, t, f"act {s}", "decay")
                    need(dve, t, f"pool {s}", STEPS[f"pool {s}"][-1], back=1)
                    v.tensor_tensor_scan(carry[l][u][:], vin[l][u][:, 0:W], dec[l][u][:], 0.0,
                                         ALU.add, ALU.mult).then_inc(me, 1)
                if ph == 4:
                    o = made_by("s")
                    tt(banks(base[l][u][:], nb), o, banks(du[l][u][:], nb), ALU.mult).then_inc(me, 1)
                    need(dve, t, f"dve {s}", "base")
                    stt(base[l][u][:], xs[l][u][:], d_col[:, l:l + 1], base[l][u][:],
                        ALU.mult, ALU.add).then_inc(me, 1)
                if ph == 5:
                    o = made_by("c")
                    need(dve, t, f"dve {s}", "scan")
                    tt(banks(carry[l][u][:], nb), o, banks(carry[l][u][:], nb), ALU.mult).then_inc(
                        sem("gen_first") if general else me, 1)

            def norm(t, s, ph, h):
                w, me = s[0], done[f"dve {s}"]
                if ph == 0:
                    need(dve, t, f"pe {s}", "mean")
                    tt(cen[w][:], h[:], ring[:, t.slot(s, "mean"), 0, 0:COLS], ALU.subtract).then_inc(me, 1)
                if ph == 1:
                    need(dve, t, f"act {s}", "rstd")
                    need(dve, t, f"pe {s}", "v" if w == "a" else f"h1_{NEP - 1}", back=1)
                    tt(nrm[w][:], cen[w][:], rstd[w][:], ALU.mult).then_inc(me, 1)

            def attention(t, s, ph):
                norm(t, s, ph, h_in)
                me = done["dve att"]
                if ph == 2:
                    need(dve, t, "pe att", "qk")
                    need(dve, t, "pe att", "s31", back=1)
                    need(dve, t, "pool att", "qe", back=1)
                    for b in range(2):
                        ts(qk[:, b], ring[:, t.slot(s, "qk"), b, 0:COLS], bqk_col[:, b:b + 1], None,
                           ALU.add).then_inc(me, 1)
                if ph == 3:
                    need(dve, t, "pe att", "n2")
                    for b, eps in ((0, NORM_EPS ** 2 / SCALE2), (1, NORM_EPS ** 2)):
                        ts(qk_sq[:, b], ring[:, t.slot(s, "n2"), b, 0:COLS], eps, None,
                           ALU.max).then_inc(me, 1)
                    need(dve, t, "act att", "rnorm")
                    tt(qk[:], qk[:], qk_sq[:], ALU.mult).then_inc(me, 1)
                if ph == 4:
                    need(dve, t, "pe att", "v")
                    need(dve, t, "pe att", "y3", back=1)
                    src = ring[0:TOUT, t.slot(s, "v"), 0, :].rearrange("m (q h d) -> m q h d", q=NPAIR, d=HD)
                    bias = bv_row[:].rearrange("m k (h d) -> m (k h) d", d=HD)[:, None, :, :].broadcast_to(
                        [TOUT, NPAIR, 2 * H, HD])
                    tt(v1[:, :, :, 1:], src, bias, ALU.add).then_inc(me, 1)
                if 6 <= ph <= 9:
                    q = ph - 6
                    need(dve, t, "pe att", f"y{q}")
                    need(dve, t, "pe att", "aT", back=1)
                    y = ring[0:TOUT, t.slot(s, f"y{q}"), 0, 0:2 * H * (HD + 1)].rearrange(
                        "m (h d) -> m h d", d=HD + 1)
                    v.reciprocal(y_rec[:, q, :], y[:, :, 0]).then_inc(me, 1)
                    need(dve, t, "dve att", f"rec{q}")
                    tt(att[:, q], y[:, :, 1:], y_rec[:, q, :, None].broadcast_to([TOUT, 2 * H, HD]),
                       ALU.mult).then_inc(me, 1)
                if ph == LASTP:
                    need(dve, t, "pe att", "proj")
                    need(dve, t, "pe ffn", "o", group=t.group(s) - 1)
                    stt(h_mid[:], ring[:, t.slot(s, "proj"), 0, 0:COLS], bp_col[:, 0:1], h_in[:],
                        ALU.add, ALU.add).then_inc(me, 1)

            def spread(col):
                return col[:, :, None].broadcast_to([TOUT, GB, NX])

            def experts(t, s, ph):
                norm(t, s, ph, h_mid)
                me = done["dve ffn"]

                def step(ins, name):
                    ins.then_inc(me, 1)
                    need(dve, t, "dve ffn", name)

                if ph == 3:
                    need(dve, t, "pe ffn", "lg")
                    src = ring[0:TOUT, t.slot(s, "lg"), 0, 0:GB * NX].rearrange("m (b e) -> m b e", e=NX)
                    step(tt(lg[:], src, rb2_row[:, None, :].broadcast_to([TOUT, GB, NX]), ALU.add), "lg")
                    step(v.tensor_reduce(st[:, 0], lg[:], AX_X, ALU.max), "mx")
                    step(tt(lg[:], lg[:], spread(st[:, 0]), ALU.subtract), "shift")
                    need(dve, t, "act ffn", "prexp")
                    step(v.tensor_reduce(st[:, 1], pr[:], AX_X, ALU.add), "sum")
                    step(v.reciprocal(st[:, 2], st[:, 1]), "rsum")
                    step(tt(pr[:], pr[:], spread(st[:, 2]), ALU.mult), "pr")
                    for k in range(2):
                        m = st[:, 3 + k]
                        step(v.tensor_reduce(m, pr[:], AX_X, ALU.max), f"m{k}")
                        step(tt(key[:], pr[:], spread(m), ALU.is_ge), f"eq{k}")
                        step(tt(key[:], key[:], rank[:], ALU.mult), f"key{k}")
                        step(v.tensor_reduce(st[:, 7], key[:], AX_X, ALU.max), f"kmax{k}")
                        step(tt(oh[k][:], key[:], spread(st[:, 7]), ALU.is_equal), f"oh{k}")
                        if k == 0:
                            step(stt(pr[:], oh[0][:], -4.0, pr[:], ALU.mult, ALU.add), "rest")
                    step(tt(st[:, 5], st[:, 4], st[:, 3], ALU.subtract), "diff")
                    need(dve, t, "act ffn", "topexp")
                    step(ts(st[:, 0], st[:, 6], 1.0, None, ALU.add), "den")
                    step(v.reciprocal(st[:, 1], st[:, 0]), "r0")
                    step(tt(st[:, 2], st[:, 1], st[:, 6], ALU.mult), "r1")
                    step(tt(oh[0][:], oh[0][:], spread(st[:, 1]), ALU.mult), "g0")
                    step(tt(oh[1][:], oh[1][:], spread(st[:, 2]), ALU.mult), "g1")
                    step(tt(gate[:], oh[0][:], oh[1][:], ALU.add), "gate")
                k = ph - 6
                if 0 <= k < NEP:
                    need(dve, t, "pe ffn", f"g_{k}")
                    need(dve, t, "act ffn", f"hid2_{k}")
                    tt(hidw[k][:], hid2[:], ring[:, t.slot(s, f"g_{k}"), :, 0:COLS], ALU.mult).then_inc(me, 1)

            def do(t, s, ph):
                {"L": ssm, "a": attention, "f": experts}[s[0]](t, s, ph)

            def do_general(t, s, ph):
                if s[0] == "L":
                    ssm(t, s, ph, general=True)
                else:
                    do(t, s, ph)
                if s[0] == "L" and ph == 5:
                    l, u = layer_unit(s)
                    nb, W = NBANK[l], NBANK[l] * COLS
                    scale = 0.5 if l < LAYERS - 1 else 1.0
                    done_before = t.k * (4 * (NS - 1)) + (l + u + (1 if l else 0)) * (NS - 1)
                    ob = ring[:, t.slot(s, "b"), 0:nb, 0:COLS]
                    oc = ring[:, t.slot(s, "c"), 0:nb, 0:COLS]
                    q, w = sem("gen_w_steps"), sem("gen_steps")
                    with dve.Fori(1, NS) as n:
                        at = done_before + n - 1
                        ts(gen_w[:, 0], blk[:], wT[:, l, bass.ds(n, 1)], None, ALU.mult).then_inc(q, 1)
                        ts(gen_w[:, 1], blk[:], wT[:, l, bass.ds(n + NS, 1)], scale, ALU.mult, ALU.mult).then_inc(q, 1)
                        dve.wait_ge(q, at * 2 + 2)
                        v.tensor_copy(gen_a[:], decay[:, l, bass.ds(n, 1)]).then_inc(sem("gen_weights"), 1)
                        dve.wait_ge(sem("gen_bc"), at + 1)
                        dve.wait_ge(sem("gen_decay"), at + 1)
                        tt(banks(vin[l][u][:, 1:W + 1], nb), ob, banks(du[l][u][:], nb), ALU.mult).then_inc(w, 1)
                        dve.wait_ge(w, at * 4 + 1)
                        v.tensor_tensor_scan(soft[l][u][:], vin[l][u][:, 0:W], dec[l][u][:], 0.0,
                                             ALU.add, ALU.mult).then_inc(w, 1)
                        dve.wait_ge(w, at * 4 + 2)
                        tt(banks(soft[l][u][:], nb), oc, banks(soft[l][u][:], nb), ALU.mult).then_inc(w, 1)
                        dve.wait_ge(w, at * 4 + 3)
                        tt(carry[l][u][:], carry[l][u][:], soft[l][u][:], ALU.add).then_inc(w, 1)
                        dve.wait_ge(w, at * 4 + 4)
                    v.memset(zero_col[:], 0.0).then_inc(done[f"dve {s}"], 1)

            walk(dve, do)
            for s in ("L0u0", "L0u1", "L1", "L2"):
                dve.wait_ge(done[f"pool {s}"], NG * len(STEPS[f"pool {s}"]))
            v.tensor_reduce(flag_sum[:], flags[:], AX_X, ALU.add).then_inc(sem("flag_sum"), 1)
            dve.wait_ge(sem("flag_pe"), 1)
            ts(flag_i[:], ring[0:1, 0, 0, 0:1], 0.0, None, ALU.is_gt).then_inc(prep["flag"], 1)
            dve.wait_ge(prep["flag"], 1)
            again = dve.value_load(flag_i[0:1, 0:1], min_val=0, max_val=1)
            with dve.If(again != 0):
                walk_general(dve, do_general)


_INS = ["x", "L0_tok_A_log", "L0_tok_D", "L0_tok_W_dbc", "L0_tok_W_dt", "L0_tok_b_dt", "L0_attn_Wqkv",
        "L0_attn_bqkv", "L0_attn_Wproj", "L0_attn_bproj", "L0_attn_temperature", "L0_ffn_router_w1",
        "L0_ffn_router_b1", "L0_ffn_router_w2", "L0_ffn_router_b2", "L0_ffn_expert_w1", "L0_ffn_expert_b1",
        "L0_ffn_expert_w2", "L0_ffn_expert_b2", "L0_ffn_expert_w3", "L0_ffn_expert_b3"]
_OUTS = [((128, 93, 64), "float32")]


def kernel(**inputs):
    import numpy as _np
    import concourse.bacc as _bacc
    from concourse import mybir as _mybir
    from concourse.bass_utils import run_bass_kernel_spmd as _run

    nc = _bacc.Bacc("TRN2", target_bir_lowering=False, num_devices=1)
    arrays, args = {}, []
    for name in _INS:
        a = _np.ascontiguousarray(inputs[name])
        arrays[f"in_{name}_dram"] = a
        args.append(nc.dram_tensor(f"in_{name}_dram", a.shape, _mybir.dt.from_np(a.dtype), kind="ExternalInput").ap())
    for i, (shape, dtype) in enumerate(_OUTS):
        dt = _mybir.dt.from_np(_np.dtype(dtype))
        args.append(nc.dram_tensor(f"out_{i}_dram", shape, dt, kind="ExternalOutput").ap())
    audio_tower(nc, *args)
    r = _run(nc, [arrays], core_ids=[0])
    got = tuple(r.results[0][f"out_{i}_dram"] for i in range(len(_OUTS)))
    return got[0]
```

```python
from contextlib import ExitStack

import concourse.bass as bass
from concourse import mybir

ALU = mybir.AluOpType
ACT = mybir.ActivationFunctionType
F32 = mybir.dt.float32
BF16 = mybir.dt.bfloat16
I32 = mybir.dt.int32
AX_X = mybir.AxisListType.X

P = 128
UNDERFLOW = -87.5
CLAMP = 40.0
LN_EPS = 1e-5
NORM_EPS = 1e-12
LN2 = 0.6931471805599453


def audio_tower(nc, x, A_log, Dp, W_dbc, W_dt, b_dt, Wqkv, bqkv, Wproj, bproj, temperature,
                r_w1, r_b1, r_w2, r_b2, e_w1, e_b1, e_w2, e_b2, e_w3, e_b3, out):
    NBATCH, _, E = x.shape
    LAYERS, _, NS = A_log.shape
    H = temperature.shape[1]
    HD = E // H
    NX, _, HID = e_w1.shape
    RH = r_w1.shape[1]
    TOUT = out.shape[1]
    T = [TOUT << (LAYERS - 1 - l) for l in range(LAYERS)]
    GB = 8
    NPAIR = GB // 2
    NG = NBATCH // GB
    COLS = 4 * TOUT
    UNITS = [2, 1, 1]
    NBANK = [2, 2, 1]
    XJ = 3
    XP = T[0] // XJ
    NEP = NX // 2
    SCALE2 = float(HD) ** 0.5
    assert 2 * E == P and NS == 64 and COLS <= 512 and XP <= P and LAYERS == 3

    ctx = ExitStack()
    with ctx:
        def sb(name, shape, dt=F32):
            return ctx.enter_context(nc.sbuf_tensor(name, shape, dt))

        sems = {}

        def sem(name):
            if name not in sems:
                sems[name] = ctx.enter_context(nc.semaphore(name))
            return sems[name]

        NSLOT = 4
        ring = ctx.enter_context(nc.psum_tensor("ring", [P, NSLOT, 2, 512], F32))

        ident = sb("ident", [P, P])
        blk = sb("blk", [P, P])
        blk_half = sb("blk_half", [P, P])
        blk_mean = sb("blk_mean", [P, P])
        blk_head = sb("blk_head", [P, P])
        ident_bf = sb("ident_bf", [TOUT, TOUT], BF16)
        four = sb("four", [TOUT, 1])
        blk_norm = sb("blk_norm", [P, P])
        zero_col = sb("zero_col", [P, 1])
        clamp_col = sb("clamp_col", [P, 1])
        under_col = sb("under_col", [P, 1])
        two_col = sb("two_col", [P, 1])
        ln_col = sb("ln_col", [P, 1])
        eps_col = sb("eps_col", [P, 1])
        rank = sb("rank", [TOUT, GB, NX])
        w_bc = sb("w_bc", [P, LAYERS, 2, E])
        w_c0 = sb("w_c0", [NS, LAYERS, 2, E])
        w_d = sb("w_d", [1, LAYERS, 2, E])
        w_t = sb("w_t", [1, LAYERS, 2, E])
        wT = sb("wT", [P, LAYERS, 2 * NS])
        m_quad = sb("m_quad", [P, LAYERS, P])
        m_delta = sb("m_delta", [P, LAYERS, P])
        m_b0 = sb("m_b0", [P, LAYERS, P])
        m_c0 = sb("m_c0", [P, LAYERS, P])
        decay = sb("decay", [P, LAYERS, NS])
        decay_max = sb("decay_max", [P, LAYERS])
        d_col = sb("d_col", [P, LAYERS])
        bdt_col = sb("bdt_col", [P, LAYERS])
        nbdt_col = sb("nbdt_col", [P, LAYERS])
        wqkv_in = sb("wqkv_in", [P, 2, E])
        wv_in = sb("wv_in", [E, 2, E])
        wp_in = sb("wp_in", [E, 2, 4, 32])
        wq_bd = sb("wq_bd", [P, P])
        wk_bd = sb("wk_bd", [P, P])
        wv_bd = sb("wv_bd", [P, P])
        wp_t = sb("wp_t", [P, 2, E])
        bqk_col = sb("bqk_col", [P, 2])
        bv_row = sb("bv_row", [TOUT, 2, E])
        bp_col = sb("bp_col", [P, 1])
        temp_col = sb("temp_col", [P, 1])
        head16 = sb("head16", [P, 16])
        mask_q = sb("mask_q", [P, 4])
        rw1 = sb("rw1", [P, 2 * RH])
        rb1_col = sb("rb1_col", [2 * RH, 1])
        rw2 = sb("rw2", [2 * RH, 2, NX])
        rb2_row = sb("rb2_row", [TOUT, NX])
        w1 = sb("w1", [P, NX, HID])
        w2 = sb("w2", [P, NEP, P])
        w3 = sb("w3", [P, NEP, E])
        b1_col = sb("b1_col", [P, NEP])
        b2_col = sb("b2_col", [P, NEP])
        b3 = sb("b3", [3 * 32, 2, E])
        b3_rest = sb("b3_rest", [3 * 32, 2, E])
        b3_part = [sb(f"b3_part{i}", [3 * 32, 2, E], BF16) for i in range(3)]
        sel = sb("sel", [3 * 32, 2, NEP, P], BF16)

        def per_unit(name, l, extra=0):
            return [sb(f"{name}{l}_{u}", [P, NBANK[l] * COLS + extra]) for u in range(UNITS[l])]

        xin = [sb(f"xin{u}", [XP, 2, XJ, 2, E]) for u in range(2)]
        xs = [per_unit("x", l) for l in range(LAYERS)]
        soft = [per_unit("soft", l) for l in range(LAYERS)]
        delta = [per_unit("delta", l) for l in range(LAYERS)]
        du = [per_unit("du", l) for l in range(LAYERS)]
        dec = [per_unit("dec", l) for l in range(LAYERS)]
        vin = [per_unit("vin", l, 1) for l in range(LAYERS)]
        carry = [per_unit("carry", l) for l in range(LAYERS)]
        base = [per_unit("base", l) for l in range(LAYERS)]
        flag_new = sb("flag_new", [P, 4])
        flags = sb("flags", [P, 4])
        gen_w = sb("gen_w", [P, 2, P])
        gen_a = sb("gen_a", [P, 1])

        h_in = sb("h_in", [P, COLS])
        h_mid = sb("h_mid", [P, COLS])
        cen = {s: sb(f"cen_{s}", [P, COLS]) for s in "af"}
        nrm = {s: sb(f"nrm_{s}", [P, COLS]) for s in "af"}
        rstd = {s: sb(f"rstd_{s}", [P, COLS]) for s in "af"}
        qk = sb("qk", [P, 2, COLS])
        qk_sq = sb("qk_sq", [P, 2, COLS])
        q_exp = sb("q_exp", [P, NPAIR, 4, TOUT])
        KROW = 96
        v1 = sb("v1", [KROW + 1, NPAIR, 2 * H, 32])
        pm = [[sb(f"pm{b}{h}", [KROW + 1, 2, 4, TOUT]) for h in range(2)] for b in range(2)]
        yT = [sb(f"yT{b}", [P, COLS]) for b in range(2)]
        y_rec = [sb(f"y_rec{b}", [P, COLS]) for b in range(2)]
        attT = sb("attT", [P, NPAIR, 4, TOUT])
        rh = sb("rh", [2 * RH, COLS])
        lg = sb("lg", [TOUT, GB, NX])
        pr = sb("pr", [TOUT, GB, NX])
        key = sb("key", [TOUT, GB, NX])
        oh = [sb(f"oh{k}", [TOUT, GB, NX]) for k in range(2)]
        st = sb("st", [TOUT, 8, GB])
        gate = sb("gate", [TOUT, GB, NX])
        gate_rest = sb("gate_rest", [TOUT, NPAIR, 2 * NX])
        gate_part = sb("gate_part", [TOUT, NPAIR, 3, 32], BF16)
        gateT = sb("gateT", [3 * 32, COLS], BF16)
        fin = sb("fin", [P, COLS])
        hid1 = sb("hid1", [P, 2, COLS])
        hid2 = sb("hid2", [P, 2, COLS])
        hidw = [sb(f"hidw{k}", [P, 2, COLS]) for k in range(NEP)]
        osb = sb("osb", [TOUT, GB, E])
        flag_f = sb("flag_f", [1, 1])
        flag_sum = sb("flag_sum", [P, 1])
        flag_i = sb("flag_i", [1, 1], I32)

        STAGES = [("ffn", 4), ("att", 3), ("L2", 2), ("L1", 1), ("L0u0", 0), ("L0u1", 0)]
        BEHIND = dict(STAGES)
        DEPTH = max(BEHIND.values())
        LASTP = 12
        SSM_JOBS = {1: [("dpre", "dve delta")], 2: [("z", "dve quad")], 3: [("b", "dve vin")],
                    4: [("s", "dve base")], 5: [("c", "dve carry")]}
        L0_JOBS = {0: [("xT", "act x")], **SSM_JOBS}
        JOBS = {
            "L0u0": L0_JOBS, "L0u1": L0_JOBS, "L1": SSM_JOBS, "L2": SSM_JOBS,
            "att": {0: [("mean", "dve cen")], 1: [("var", "act ln")], 2: [("qk", "dve k")], 3: [("n2", "dve rk")],
                    4: [("v", "dve v1")], 5: [("vs", "act vrow"), ("s00", "act pm00"), ("s01", "act pm01")],
                    6: [("s10", "act pm10"), ("s11", "act pm11"), ("y0", "act yT0")],
                    7: [("s20", "act pm20"), ("s21", "act pm21"), ("y1", "act yT1"), ("nb0", "act nln0")],
                    8: [("s30", "act pm30"), ("s31", "act pm31"), ("y2", "act yT2"), ("nb1", "act nln1")],
                    9: [("y3", "act yT3"), ("nb2", "act nln2")], 10: [("nb3", "act nln3")],
                    LASTP: [("proj", "dve mid")]},
            "ffn": {0: [("mean", "dve cen")], 1: [("var", "act ln")], 2: [("rh", "act rh")], 3: [("lg", "dve lg")],
                    5: [("h1_0", "act hid1_0")],
                    6: [("h2_0", "act hid2_0"), ("h1_1", "act hid1_1"), ("gT", "act gateT")],
                    7: [("g_0", "dve hidw0"), ("h2_1", "act hid2_1"), ("h1_2", "act hid1_2")],
                    8: [("g_1", "dve hidw1"), ("h2_2", "act hid2_2")], 9: [("g_2", "dve hidw2")],
                    10: [("o", "dve fin")], 11: [("oT", "act out")]},
        }
        SSM_ACT = ["relu", "exp", "ln", "alive", "decay"]
        SSM_DVE = ["delta", "quad", "vin", "scan", "base", "based", "carry"]
        SSM_POOL = ["du", "flag", "y", "pooled"]
        STEPS = {f"pe {s}": [j for ph in sorted(JOBS[s]) for j, _ in JOBS[s][ph]] for s, _ in STAGES}
        for s_ in ("L0u0", "L0u1", "L1", "L2"):
            STEPS[f"act {s_}"] = (["x"] if s_[:2] == "L0" else []) + SSM_ACT
            STEPS[f"dve {s_}"] = SSM_DVE
            STEPS[f"pool {s_}"] = SSM_POOL[:3] if s_ == "L2" else SSM_POOL
        STEPS["act att"] = ["sq", "ln", "rstd", "qksq", "lnorm", "rnorm"] + [
            "vrow", "pm00", "pm01", "pm10", "pm11", "yT0", "pm20", "pm21", "yT1", "nln0", "rec0",
            "pm30", "pm31", "yT2", "nln1", "rec1", "yT3", "nln2", "rec2", "nln3", "rec3"]
        STEPS["dve att"] = ["cen", "hn", "q", "k", "rq", "rk", "hat", "v1"] + \
            [f"att{q}" for q in range(4)] + ["mid"]
        STEPS["pool att"] = ["qe"]
        STEPS["pool ffn"] = ["hi", "mid", "rest", "lo"]
        STEPS["act ffn"] = ["sq", "ln", "rstd", "rh", "prexp", "hid1_0", "topexp", "hid2_0", "hid1_1", "gateT",
                            "hid2_1", "hid1_2", "hid2_2", "out"]
        ROUTE1 = ["lg", "mx", "shift", "sum", "rsum", "pr"]
        TOP = ["m", "eq", "key", "kmax", "oh"]
        ROUTE2 = [f"{w}0" for w in TOP] + ["rest"] + [f"{w}1" for w in TOP] + ["diff", "den", "r0", "r1", "g0", "g1", "gate"]
        STEPS["dve ffn"] = ["cen", "hn"] + ROUTE1 + ROUTE2 + ["hidw0", "hidw1", "hidw2", "fin"]
        STEPS["sp L0u0"] = STEPS["sp L0u1"] = [f"load{b}" for b in range(4)]
        STEPS["sp ffn"] = ["store"]
        done = {who: sem(who.replace(" ", "_")) for who in STEPS}

        START = {"ffn": 0, "att": 0, "L2": 6, "L1": 3, "L0u0": 0, "L0u1": 6}
        OVERLAPPED = [(s, at - START[s]) for at in range(2 * LASTP) for s, _ in STAGES
                      if 0 <= at - START[s] < LASTP] + [(s, LASTP) for s, _ in STAGES]
        IN_ORDER = [(s, ph) for s in ("L0u0", "L0u1", "L1", "L2", "att", "ffn") for ph in range(LASTP + 1)]

        def slots_of(order):
            jobs = [(s, j, r) for s, ph in order for j, r in JOBS[s].get(ph, ())]
            last, slots = {}, {}
            for again in (0, 1):
                for at, (s, j, r) in enumerate(jobs):
                    k = at % NSLOT
                    earlier = last.get(k)
                    slots[s, j] = (k, earlier and (*earlier[:2], earlier[2] < again))
                    last[k] = (s, r, again)
            return slots, jobs

        class Turn:

            def __init__(self, order, first, k, overlapped):
                self.first, self.k, self.overlapped = first, k, overlapped
                self.live = [s for s, b in STAGES if not overlapped or not isinstance(first, int)
                             or 0 <= first - b < NG]
                self.order = [(s, ph) for s, ph in order if s in self.live]
                self.slots, self.jobs = slots_of(order)

            def group(self, s):
                return self.k + (self.first - BEHIND[s]) if self.overlapped else self.k + NG

            def batch(self, s):
                return self.group(s) if self.overlapped else self.k

            def slot(self, s, job):
                return self.slots[s, job][0]

        def need(eng, t, who, step, group=None, back=0):
            g = (t.group(who.split()[1]) if group is None else group) - back
            steps = STEPS[who]
            by = 16 if who[:2] == "sp" else 1
            if isinstance(g, int):
                if g < 0:
                    return
            eng.wait_ge(done[who], g * (by * len(steps)) + by * (steps.index(step) + 1))

        def slot_for(eng, t, s, job):
            k, earlier = t.slots[s, job]
            es, er, turn_before = earlier
            if isinstance(t.group(es), int):
                at = [(a, b) for a, b, _ in t.jobs].index((s, job))
                for i in range(at - 1, at - 4 * len(t.jobs), -1):
                    a, _, r = t.jobs[i % len(t.jobs)]
                    g = t.group(a) + i // len(t.jobs)
                    if i % len(t.jobs) % NSLOT == k and 0 <= g < NG:
                        need(eng, t, f"{r.split()[0]} {a}", r.split()[1], group=g)
                        break
            else:
                need(eng, t, f"{er.split()[0]} {es}", er.split()[1], group=t.group(es) - turn_before)
            return ring[:, k]

        def walk(eng, do):
            def turn(t):
                for s, ph in t.order:
                    do(t, s, ph)
            for i in range(DEPTH + 1):
                turn(Turn(OVERLAPPED, i, 0, True))
            with eng.Fori(0, NG - DEPTH - 1) as k:
                t = Turn(OVERLAPPED, DEPTH + 1, k, True)
                turn(t)
            for i in range(NG, NG + DEPTH):
                turn(Turn(OVERLAPPED, i, 0, True))

        def walk_general(eng, do):
            with eng.Fori(0, NG) as k:
                t = Turn(IN_ORDER, 0, k, False)
                for s, ph in t.order:
                    do(t, s, ph)

        def layer_unit(s):
            return int(s[1]), int(s[3]) if len(s) > 2 else 0

        def banks(ap, n):
            return ap.rearrange("p (b c) -> p b c", b=n)

        NPREP, MASKS = 81, 16
        prep = {n: sem(f"prep_{n}") for n in ("dma", "pe", "copy", "const", "done", "exp", "flag")}
        blocks4 = [(l, k) for l in range(LAYERS) for k in range(2)]

        block = ctx.enter_context(nc.Block())

        @block.sync
        def _(sp):
            n = [0]

            def load(dst, src):
                sp.dma_start(dst, src, allow_slow_non_contiguous=True).then_inc(prep["dma"], 16)
                n[0] += 1

            def load_x(s, first):
                _, u = layer_unit(s)
                for b in range(4):
                    sp.dma_start(xin[u][:, b // 2, :, b % 2, :],
                                 x[bass.ds(first + u * 4 + b, 1), 0:T[0], :].rearrange(
                                     "b (p j) e -> p (b j) e", j=XJ)).then_inc(done[f"sp {s}"], 16)

            for l in range(LAYERS):
                for k in range(2):
                    load(w_bc[:, l, k, :], W_dbc[l, 1:1 + 2 * NS, :])
                    load(w_c0[:, l, k, :], W_dbc[l, 1 + NS:1 + 2 * NS, :])
                    load(w_d[:, l, k, :], W_dbc[l, 0:1, :])
                    load(w_t[:, l, k, :], W_dt[l, :, :].rearrange("e r -> r e"))
            load_x("L0u0", 0)
            load_x("L0u1", 0)
            for k in range(2):
                half = slice(E * k, E * k + E)
                load(decay[half, :, :], A_log.rearrange("l e n -> e l n"))
                load(d_col[half, :], Dp.rearrange("l e -> e l"))
                load(bdt_col[half, :], b_dt.rearrange("l e -> e l"))
                load(wqkv_in[:, k, :], Wqkv[0:P, :])
                load(wv_in[:, k, :], Wqkv[P:P + E, :])
                load(bqk_col[half, :], bqkv[0:P].rearrange("(c e) -> e c", c=2))
                load(bv_row[:, k, :], bqkv[P:P + E].rearrange("(a e) -> a e", a=1).broadcast_to([TOUT, E]))
                load(bp_col[half, :], bproj.rearrange("(e a) -> e a", a=1))
                for h in range(H):
                    load(temp_col[E * k + HD * h:E * k + HD * h + HD, :],
                         temperature[0, h:h + 1, :, 0].broadcast_to([HD, 1]))
                load(rb1_col[RH * k:RH * k + RH, :], r_b1.rearrange("(e a) -> e a", a=1))
                load(w1[half, :, :], e_w1.rearrange("x d h -> d x h"))
                load(w3[half, :, :], e_w3.rearrange("(c k) h o -> k h c o", k=2)[k])
                load(b1_col[half, :], e_b1.rearrange("(c k) h -> k h c", k=2)[k])
                load(b2_col[half, :], e_b2.rearrange("(c k) h -> k h c", k=2)[k])
            load(rb2_row[:], r_b2.rearrange("(a e) -> a e", a=1).broadcast_to([TOUT, NX]))
            sp.wait_ge(prep["const"], 5)
            for k in range(2):
                half = slice(E * k, E * k + E)
                load(rw1[half, RH * k:RH * k + RH], r_w1)
                load(rw2[RH * k:RH * k + RH, k, :], r_w2)
                load(w2[half, :, half], e_w2.rearrange("(c k) h f -> k h c f", k=2)[k])
                for i in range(3):
                    at = 32 * i + NX * k
                    load(b3[at:at + NX, k, :], e_b3)
                load(wp_in[:, k, :, 1:HD + 1], Wproj[:, 4 * HD * k:4 * HD * (k + 1)].rearrange("c (j d) -> c j d", j=4))
            assert n[0] == NPREP

            def do(t, s, ph):
                if s[:2] == "L0" and ph == 0:
                    g = t.group(s)
                    if isinstance(g, int) and g == 0:
                        return
                    need(sp, t, f"pe {s}", "xT", back=1)
                    load_x(s, t.batch(s) * GB)
                if s == "ffn" and ph == LASTP:
                    need(sp, t, "act ffn", "out")
                    sp.dma_start(out[bass.ds(t.batch(s) * GB, GB), :, :].rearrange("b t e -> t b e"),
                                 osb[:]).then_inc(done["sp ffn"], 16)

            walk(sp, do)
            sp.wait_ge(done["sp ffn"], 16 * NG)
            sp.wait_ge(prep["flag"], 1)
            again = sp.value_load(flag_i[0:1, 0:1], min_val=0, max_val=1)
            with sp.If(again != 0):
                walk_general(sp, do)
                sp.wait_ge(done["sp ffn"], 32 * NG)

        @block.gpsimd
        def _(pool):
            g = nc.gpsimd
            cst = sem("masks")
            g.memset(ident[:], 0.0).then_inc(cst, 1)
            g.memset(sel[:], 0.0).then_inc(cst, 1)
            g.memset(blk_head[:], 1.0).then_inc(cst, 1)
            g.memset(head16[:], 1.0).then_inc(cst, 1)
            g.memset(blk_norm[:], 0.0).then_inc(cst, 1)
            pool.wait_ge(cst, 5)
            g.affine_select(out=ident[:], in_=ident[:], compare_op=ALU.not_equal, fill=1.0, base=0,
                            pattern=[[-1, P]], channel_multiplier=1).then_inc(cst, 1)
            sv = sel[:].rearrange("r a b (x m) -> r (a b x) m", x=2)
            for i in range(3):
                g.affine_select(out=sv, in_=sv, compare_op=ALU.not_equal, fill=1.0, base=-32 * i,
                                pattern=[[-1, 2 * NX], [0, HID]], channel_multiplier=1).then_inc(cst, 1)
                pool.wait_ge(cst, 7 + i)
            nv = blk_norm[:].rearrange("p (a c) -> p a c", c=32)
            g.affine_select(out=nv, in_=nv, compare_op=ALU.not_equal, fill=1.0, base=0,
                            pattern=[[-32, 4], [0, 32]], channel_multiplier=1).then_inc(cst, 1)
            g.tensor_copy(ident_bf[:], ident[0:TOUT, 0:TOUT]).then_inc(cst, 1)
            for off, mult in ((0, 1), (HD - 1, -1)):
                for t_, c in ((blk_head, HD), (head16, 1)):
                    v = t_[:].rearrange("p (a c) -> p a c", c=c)
                    g.affine_select(out=v, in_=v, compare_op=ALU.is_ge, fill=0.0, base=off,
                                    pattern=[[-HD * mult, P // HD], [0, c]],
                                    channel_multiplier=mult).then_inc(cst, 1)
                pool.wait_ge(cst, 13 if mult == 1 else 15)
            g.memset(flags[:], 0.0).then_inc(cst, 1)
            pool.wait_ge(cst, MASKS)
            pool.wait_ge(prep["done"], 1)

            def ssm(t, s, ph):
                l, u = layer_unit(s)
                me = done[f"pool {s}"]
                f = u if l == 0 else l + 1
                if ph == 1:
                    need(pool, t, f"dve {s}", "delta")
                    g.tensor_tensor(du[l][u][:], delta[l][u][:], xs[l][u][:], ALU.mult).then_inc(me, 1)
                if ph == 2:
                    need(pool, t, f"act {s}", "alive")
                    need(pool, t, f"pool {s}", "flag", back=1)
                    g.tensor_tensor(flags[:, f:f + 1], flags[:, f:f + 1], flag_new[:, f:f + 1],
                                    ALU.add).then_inc(me, 1)
                if ph == LASTP:
                    need(pool, t, f"dve {s}", "carry")
                    if l == LAYERS - 1:
                        need(pool, t, "dve att", "mid", group=t.group(s) - 1)
                        g.tensor_tensor(h_in[:], base[l][u][:], carry[l][u][:], ALU.add).then_inc(me, 1)
                        return
                    g.tensor_tensor(base[l][u][:], base[l][u][:], carry[l][u][:], ALU.add).then_inc(me, 1)
                    need(pool, t, f"pool {s}", "y")
                    need(pool, t, f"dve L{l + 1}", "carry", group=t.group(s) - 1)
                    pairs = base[l][u][:].rearrange("p (t two) -> p t two", two=2)
                    half = NBANK[l] * COLS // 2
                    g.tensor_tensor(xs[l + 1][0][:, u * half:(u + 1) * half], pairs[:, :, 0], pairs[:, :, 1],
                                    ALU.add).then_inc(me, 1)

            def do(t, s, ph):
                if s[0] == "L":
                    ssm(t, s, ph)
                if s == "att" and ph == 3:
                    need(pool, t, "dve att", "hat")
                    need(pool, t, "pe att", "s31", back=1)
                    wide = [P, NPAIR, 4, TOUT]
                    g.tensor_tensor(q_exp[:],
                                    qk[:, 0, :].rearrange("p (q t) -> p q t", q=NPAIR)[:, :, None, :].broadcast_to(wide),
                                    mask_q[:, None, :, None].broadcast_to(wide), ALU.mult).then_inc(done["pool att"], 1)

                if s == "ffn" and ph == 6:
                    me = done["pool ffn"]
                    src = gate[:].rearrange("m (q h) e -> m q (h e)", h=2)
                    need(pool, t, "dve ffn", "gate")
                    need(pool, t, "pe ffn", "gT", back=1)
                    part = [gate_part[:, :, i, 0:2 * NX] for i in range(3)]
                    one, other = (o_[:].rearrange("m (q h) e -> m q (h e)", h=2) for o_ in oh)
                    g.tensor_tensor(part[0], one, other, ALU.add).then_inc(me, 1)
                    need(pool, t, "pool ffn", "hi")
                    g.tensor_tensor(part[1], src, part[0], ALU.subtract).then_inc(me, 1)
                    g.tensor_tensor(gate_rest[:], src, part[0], ALU.subtract).then_inc(me, 1)
                    need(pool, t, "pool ffn", "rest")
                    g.tensor_tensor(part[2], gate_rest[:], part[1], ALU.subtract).then_inc(me, 1)

            walk(pool, do)
            pool.wait_ge(prep["flag"], 1)
            again = pool.value_load(flag_i[0:1, 0:1], min_val=0, max_val=1)
            with pool.If(again != 0):
                walk_general(pool, do)

        @block.scalar
        def _(act):
            a = nc.scalar
            a.preload_act_table_set("natural_log_exp_and_others")
            act.wait_ge(prep["dma"], 16 * NPREP)
            a.activation(decay[:], decay[:], ACT.Exp).then_inc(prep["exp"], 1)
            act.wait_ge(prep["done"], 1)

            def ssm(t, s, ph):
                l, u = layer_unit(s)
                nb = NBANK[l]
                me = done[f"act {s}"]
                buf = soft[l][u][:]
                f = u if l == 0 else l + 1
                if ph == 0 and l == 0:
                    need(act, t, f"pe {s}", "xT")
                    need(act, t, f"dve {s}", "carry", back=1)
                    a.activation(banks(xs[0][u][:], nb), ring[:, t.slot(s, "xT"), 0:nb, 0:COLS],
                                 ACT.Copy).then_inc(me, 1)
                if ph == 1:
                    need(act, t, f"pe {s}", "dpre")
                    need(act, t, f"dve {s}", "carry", back=1)
                    a.activation(banks(buf, nb), ring[:, t.slot(s, "dpre"), 0:nb, 0:COLS], ACT.Relu,
                                 bias=nbdt_col[:, l:l + 1], scale=-1.0).then_inc(me, 1)
                    need(act, t, f"act {s}", "relu")
                    a.activation(buf, buf, ACT.Exp, bias=clamp_col[:], scale=-1.0).then_inc(me, 1)
                    need(act, t, f"act {s}", "exp")
                    a.activation(buf, buf, ACT.Ln, bias=1.0).then_inc(me, 1)
                if ph == 2:
                    need(act, t, f"dve {s}", "delta")
                    need(act, t, f"pool {s}", "flag", back=1)
                    dl = delta[l][u][:].rearrange("p (q t) -> p q t", t=T[l])[:, :, 1:]
                    dc = dec[l][u][:].rearrange("p (q t) -> p q t", t=T[l])[:, :, 1:]
                    a.activation(dc, dl, ACT.Relu, bias=under_col[:], scale=decay_max[:, l:l + 1],
                                 accum_out=flag_new[:, f:f + 1]).then_inc(me, 1)
                    need(act, t, f"act {s}", "alive")
                    a.activation(dc, dl, ACT.Exp, scale=decay[:, l, 0:1]).then_inc(me, 1)

            def norm(t, s, ph):
                w, me = s[0], done[f"act {s}"]
                if ph == 0:
                    need(act, t, f"dve {s}", "cen")
                    a.activation(rstd[w][:], cen[w][:], ACT.Square).then_inc(me, 1)
                if ph == 1:
                    need(act, t, f"pe {s}", "var")
                    a.activation(rstd[w][:], ring[:, t.slot(s, "var"), 0, 0:COLS], ACT.Ln,
                                 bias=eps_col[:]).then_inc(me, 1)
                    need(act, t, f"act {s}", "ln")
                    a.activation(rstd[w][:], rstd[w][:], ACT.Exp, scale=-0.5).then_inc(me, 1)

            def attention(t, s, ph):
                norm(t, s, ph)
                me = done["act att"]
                if ph == 2:
                    need(act, t, "dve att", "k")
                    a.activation(qk_sq[:], qk[:], ACT.Square).then_inc(me, 1)
                if ph == 3:
                    need(act, t, "dve att", "rk")
                    a.activation(qk_sq[:], qk_sq[:], ACT.Ln, scale=2.0 ** 24).then_inc(me, 1)
                    need(act, t, "act att", "lnorm")
                    a.activation(qk_sq[:], qk_sq[:], ACT.Exp, bias=ln_col[:], scale=-0.5).then_inc(me, 1)
                if ph == 5:
                    need(act, t, "pe att", "vs")
                    for b in range(2):
                        ins = a.activation(v1[KROW:KROW + 1, 2 * b:2 * b + 2, :, 0:HD + 1].rearrange("o q h d -> o (q h) d"),
                                           ring[KROW:KROW + 1, t.slot(s, "vs"), b, 0:4 * H * (HD + 1)].rearrange(
                                               "o (h d) -> o h d", d=HD + 1), ACT.Copy)
                    ins.then_inc(me, 1)
                if 5 <= ph <= 8:
                    q = ph - 5
                    for h in range(2):
                        need(act, t, "pe att", f"s{q}{h}")
                        need(act, t, "pe att", f"y{(q - 2) % 4}", back=1 if q < 2 else 0)
                        a.activation(pm[q % 2][h][0:TOUT].rearrange("m a j n -> m a (j n)"),
                                     ring[0:TOUT, t.slot(s, f"s{q}{h}"), :, 0:COLS], ACT.Square,
                                     bias=two_col[0:TOUT], scale=0.5 ** 0.5).then_inc(me, 1)
                if 6 <= ph <= 9:
                    q = ph - 6
                    need(act, t, "pe att", f"y{q}")
                    need(act, t, "dve att", f"att{(q - 2) % 4}", back=1 if q < 2 else 0)
                    a.activation(yT[q % 2][:], ring[:, t.slot(s, f"y{q}"), 0, 0:COLS], ACT.Copy).then_inc(me, 1)
                if 7 <= ph <= 10:
                    q = ph - 7
                    need(act, t, "pe att", f"nb{q}")
                    need(act, t, "dve att", f"att{(q - 2) % 4}", back=1 if q < 2 else 0)
                    a.activation(y_rec[q % 2][:], ring[:, t.slot(s, f"nb{q}"), 0, 0:COLS], ACT.Ln).then_inc(me, 1)
                    need(act, t, "act att", f"nln{q}")
                    a.activation(y_rec[q % 2][:], y_rec[q % 2][:], ACT.Exp, scale=-1.0).then_inc(me, 1)

            def experts(t, s, ph):
                norm(t, s, ph)
                me = done["act ffn"]

                def relu(dst, job, bias, rows=P, nb=2):
                    need(act, t, "pe ffn", job)
                    k = t.slot(s, job)
                    src = ring[0:rows, k, :, 0:COLS] if nb == 2 else ring[0:rows, k, 0, 0:COLS]
                    a.activation(dst[:], src, ACT.Relu, bias=bias).then_inc(me, 1)

                if ph == 2:
                    relu(rh, "rh", rb1_col[:], rows=2 * RH, nb=1)
                if ph == 3:
                    need(act, t, "dve ffn", "shift")
                    a.activation(pr[:], lg[:], ACT.Exp).then_inc(me, 1)
                k = ph - 6
                if 0 <= k < NEP:
                    need(act, t, "dve ffn", f"hidw{(k - 1) % NEP}", back=0 if k else 1)
                    relu(hid2, f"h2_{k}", b2_col[:, k:k + 1])
                if 0 <= k + 1 < NEP:
                    relu(hid1, f"h1_{k + 1}", b1_col[:, k + 1:k + 2])
                if ph == 5:
                    need(act, t, "dve ffn", "diff")
                    a.activation(st[:, 6, :], st[:, 5, :], ACT.Exp).then_inc(me, 1)
                if ph == 6:
                    need(act, t, "pe ffn", "gT")
                    wide = TOUT + TOUT % 2
                    a.activation(gateT[:].rearrange("r (q n) -> r q n", q=NPAIR),
                                 ring[0:3 * 32, t.slot(s, "gT"), 0, :].bitcast(BF16)[:, 0:NPAIR * wide].rearrange(
                                     "r (q n) -> r q n", q=NPAIR)[:, :, 0:TOUT], ACT.Copy).then_inc(me, 1)
                if ph == 11:
                    need(act, t, "pe ffn", "oT")
                    need(act, t, "sp ffn", "store", back=1)
                    a.activation(osb[:].rearrange("t b e -> t (b e)"), ring[0:TOUT, t.slot(s, "oT"), 0, :],
                                 ACT.Copy).then_inc(me, 1)

            def do(t, s, ph):
                {"L": ssm, "a": attention, "f": experts}[s[0]](t, s, ph)

            def do_general(t, s, ph):
                do(t, s, ph)
                if s[0] == "L" and ph == 5:
                    l, u = layer_unit(s)
                    dl = delta[l][u][:].rearrange("p (q t) -> p q t", t=T[l])[:, :, 1:]
                    dc = dec[l][u][:].rearrange("p (q t) -> p q t", t=T[l])[:, :, 1:]
                    done_before = t.k * (4 * (NS - 1)) + (l + u + (1 if l else 0)) * (NS - 1)
                    with act.Fori(1, NS) as n:
                        act.wait_ge(sem("gen_weights"), done_before + n)
                        a.activation(dc, dl, ACT.Exp, scale=gen_a[:]).then_inc(sem("gen_decay"), 1)

            walk(act, do)
            act.wait_ge(prep["flag"], 1)
            again = act.value_load(flag_i[0:1, 0:1], min_val=0, max_val=1)
            with act.If(again != 0):
                walk_general(act, do_general)

        @block.tensor
        def _(pe):
            mm = nc.tensor.matmul

            pe.wait_ge(prep["dma"], 16 * NPREP)
            pe.wait_ge(sem("masks"), MASKS)
            for l in range(LAYERS):
                o = ring[:, l, 0]
                two = "r k e -> r (k e)"
                mm(o[:, 0:P], w_bc[0:NS, l].rearrange(two), w_c0[:, l].rearrange(two), start=True, stop=True)
                mm(o[:, P:2 * P], w_d[:, l].rearrange(two), w_t[:, l].rearrange(two), start=True, stop=True)
                nc.tensor.transpose(o[:, 2 * P:3 * P], w_bc[:, l].rearrange(two), ident[:]).then_inc(prep["pe"], 1)
            o = ring[:, 3, 0]
            nc.tensor.transpose(o[:, 0:P], wqkv_in[:].rearrange("r k e -> r (k e)"), ident[:])
            nc.tensor.transpose(o[:, P:P + E], wv_in[:].rearrange("r k e -> r (k e)"), ident[0:E, 0:E])
            for b in range(2):
                ins = nc.tensor.transpose(o[:, P + E * (b + 1):P + E * (b + 2)],
                                          wp_in[:, b].rearrange("r j d -> r (j d)"), ident[0:E, 0:E])
            ins.then_inc(prep["pe"], 1)
            pe.wait_ge(prep["done"], 1)

            def ssm(t, s, ph):
                l, u = layer_unit(s)
                nb = NBANK[l]
                me = done[f"pe {s}"]
                if ph == 0 and l == 0:
                    need(pe, t, f"sp {s}", "load3")
                    o = slot_for(pe, t, s, "xT")
                    for q in range(2):
                        for j in range(XJ):
                            ins = nc.tensor.transpose(
                                o[:, q, 0:COLS].rearrange("p (t j) -> p t j", j=XJ)[:, :, j],
                                xin[u][:, q, j].rearrange("p h e -> p (h e)"), ident[0:XP, 0:XP])
                    ins.then_inc(me, 1)
                    return
                if ph not in SSM_JOBS:
                    return
                job = SSM_JOBS[ph][0][0]
                if job == "s":
                    need(pe, t, f"dve {s}", "quad")
                    w, src = (blk_half if l < LAYERS - 1 else blk)[:], soft[l][u]
                else:
                    w = {"dpre": m_delta, "z": m_quad, "b": m_b0, "c": m_c0}[job][:, l]
                    src = xs[l][u]
                    if l == 0:
                        need(pe, t, f"act {s}", "x")
                    elif l == 1:
                        need(pe, t, "pool L0u0", "pooled", group=t.group(s))
                        need(pe, t, "pool L0u1", "pooled", group=t.group(s))
                    else:
                        need(pe, t, "pool L1", "pooled", group=t.group(s))
                o = slot_for(pe, t, s, job)
                for b in range(nb):
                    ins = mm(o[:, b, 0:COLS], w, src[:, b * COLS:(b + 1) * COLS], start=True, stop=True)
                ins.then_inc(me, 1)

            def norm(t, s, ph, h):
                me = done[f"pe {s}"]
                if ph == 0:
                    o = slot_for(pe, t, s, "mean")
                    mm(o[:, 0, 0:COLS], blk_mean[:], h[:], start=True, stop=True).then_inc(me, 1)
                if ph == 1:
                    need(pe, t, f"act {s}", "sq")
                    o = slot_for(pe, t, s, "var")
                    mm(o[:, 0, 0:COLS], blk_mean[:], rstd[s[0]][:], start=True, stop=True).then_inc(me, 1)

            def attention(t, s, ph):
                me = done["pe att"]
                hn = nrm["a"]
                if ph == 0:
                    need(pe, t, "pool L2", "y", group=t.group(s))
                norm(t, s, ph, h_in)
                if ph == 2:
                    need(pe, t, "dve att", "hn")
                    o = slot_for(pe, t, s, "qk")
                    mm(o[:, 0, 0:COLS], wq_bd[:], hn[:], start=True, stop=True)
                    mm(o[:, 1, 0:COLS], wk_bd[:], hn[:], start=True, stop=True).then_inc(me, 1)
                if ph == 3:
                    need(pe, t, "act att", "qksq")
                    o = slot_for(pe, t, s, "n2")
                    for b in range(2):
                        ins = mm(o[:, b, 0:COLS], blk_head[:], qk_sq[:, b, :], start=True, stop=True)
                    ins.then_inc(me, 1)
                if ph == 4:
                    o = slot_for(pe, t, s, "v")
                    for q in range(NPAIR):
                        ins = mm(o[0:TOUT, 0, q * P:(q + 1) * P], hn[:, q * TOUT:(q + 1) * TOUT], wv_bd[:],
                                 start=True, stop=True)
                    ins.then_inc(me, 1)
                if ph == 5:
                    need(pe, t, "dve att", "v1")
                    o = slot_for(pe, t, s, "vs")
                    for b in range(2):
                        ins = mm(o[KROW:KROW + 1, b, 0:4 * H * (HD + 1)], four[:],
                                 v1[0:TOUT, 2 * b:2 * b + 2, :, 0:HD + 1].rearrange("m q h d -> m (q h) d"),
                                 start=True, stop=True, tile_position=(0, KROW))
                    ins.then_inc(me, 1)
                if 5 <= ph <= 8:
                    q = ph - 5
                    need(pe, t, "pool att", "qe")
                    for h in range(2):
                        o = slot_for(pe, t, s, f"s{q}{h}")
                        for b in range(2):
                            r = E * h + 32 * b
                            ins = mm(o[0:TOUT, b, 0:COLS], qk[r:r + 32, 1, q * TOUT:(q + 1) * TOUT],
                                     q_exp[r:r + 32, q].rearrange("p j n -> p (j n)"), start=True, stop=True,
                                     tile_position=(r, 0))
                        ins.then_inc(me, 1)
                if 6 <= ph <= 9:
                    q = ph - 6
                    need(pe, t, "act att", "vrow")
                    need(pe, t, "act att", f"pm{q}1")
                    o = slot_for(pe, t, s, f"y{q}")
                    for h in range(2):
                        for b in range(2):
                            for j in range(4):
                                at = (2 * h + b) * TOUT
                                ins = mm(o[32 * j:32 * j + 32, 0, at:at + TOUT], v1[:, q, H * h + 4 * b + j, :],
                                         pm[q % 2][h][:, b, j, :], start=True, stop=True, tile_position=(0, 32 * j))
                    ins.then_inc(me, 1)
                if 7 <= ph <= 10:
                    q = ph - 7
                    need(pe, t, "act att", f"yT{q}")
                    o = slot_for(pe, t, s, f"nb{q}")
                    mm(o[:, 0, 0:COLS], blk_norm[:], yT[q % 2][:], start=True, stop=True).then_inc(me, 1)
                if ph == LASTP:
                    need(pe, t, "dve att", "att3")
                    o = slot_for(pe, t, s, "proj")
                    for h in range(2):
                        for b in range(2):
                            ins = mm(o[E * h:E * h + E, 0, 0:COLS].rearrange("p (q n) -> p q n", q=NPAIR),
                                     wp_t[:, b], attT[:, :, 2 * h + b, :], start=(b == 0), stop=(b == 1),
                                     tile_position=(0, E * h))
                    ins.then_inc(me, 1)

            def experts(t, s, ph):
                me = done["pe ffn"]
                hn = nrm["f"]
                if ph == 0:
                    need(pe, t, "dve att", "mid", group=t.group(s))
                norm(t, s, ph, h_mid)
                if ph == 2:
                    need(pe, t, "dve ffn", "hn")
                    o = slot_for(pe, t, s, "rh")
                    mm(o[0:2 * RH, 0, 0:COLS], rw1[:], hn[:], start=True, stop=True).then_inc(me, 1)
                if ph == 3:
                    need(pe, t, "act ffn", "rh")
                    o = slot_for(pe, t, s, "lg")
                    for q in range(NPAIR):
                        ins = mm(o[0:TOUT, 0, q * 2 * NX:(q + 1) * 2 * NX], rh[:, q * TOUT:(q + 1) * TOUT],
                                 rw2[:].rearrange("r k e -> r (k e)"), start=True, stop=True)
                    ins.then_inc(me, 1)
                k = ph - 7
                if 0 <= k < NEP:
                    need(pe, t, "act ffn", "gateT")
                    o = slot_for(pe, t, s, f"g_{k}")
                    for h in range(2):
                        ins = mm(o[:, h, 0:COLS], sel[:, h, k], gateT[:], start=True, stop=True)
                    ins.then_inc(me, 1)
                k = ph - 6
                if 0 <= k < NEP:
                    need(pe, t, "act ffn", f"hid1_{k}")
                    o = slot_for(pe, t, s, f"h2_{k}")
                    for h in range(2):
                        ins = mm(o[:, h, 0:COLS], w2[:, k], hid1[:, h], start=True, stop=True)
                    ins.then_inc(me, 1)
                if 0 <= k + 1 < NEP:
                    o = slot_for(pe, t, s, f"h1_{k + 1}")
                    for h in range(2):
                        ins = mm(o[:, h, 0:COLS], w1[E * h:E * h + E, 2 * k + 2:2 * k + 4].rearrange("p x m -> p (x m)"),
                                 hn[E * h:E * h + E, :], start=True, stop=True, tile_position=(E * h, 0))
                    ins.then_inc(me, 1)
                if ph == 6:
                    need(pe, t, "pool ffn", "lo")
                    o = slot_for(pe, t, s, "gT")[0:3 * 32, 0, :].bitcast(BF16)
                    for q in range(NPAIR):
                        at = q * (TOUT + TOUT % 2)
                        ins = nc.tensor.transpose(o[:, at:at + TOUT],
                                                  gate_part[:, q].rearrange("m i r -> m (i r)"), ident_bf[:])
                    ins.then_inc(me, 1)
                if ph == 10:
                    need(pe, t, "dve ffn", f"hidw{NEP - 1}")
                    o = slot_for(pe, t, s, "o")
                    for i in range(3):
                        mm(o[:, 0, 0:COLS], b3_part[i][:].rearrange("r h e -> r (h e)"), gateT[:],
                           start=(i == 0), stop=(i == 2))
                    for h in range(2):
                        for k in range(NEP):
                            ins = mm(o[E * h:E * h + E, 0, 0:COLS], w3[:, k], hidw[k][:, h], start=False,
                                     stop=True, skip_group_check=True, tile_position=(0, E * h))
                    ins.then_inc(me, 1)
                if ph == 11:
                    need(pe, t, "dve ffn", "fin")
                    o = slot_for(pe, t, s, "oT")
                    for q in range(NPAIR):
                        ins = nc.tensor.transpose(o[0:TOUT, 0, q * P:(q + 1) * P],
                                                  fin[:, q * TOUT:(q + 1) * TOUT], ident[:])
                    ins.then_inc(me, 1)

            def do(t, s, ph):
                {"L": ssm, "a": attention, "f": experts}[s[0]](t, s, ph)

            def do_general(t, s, ph):
                do(t, s, ph)
                if s[0] == "L" and ph == 5:
                    l, u = layer_unit(s)
                    ob, oc = ring[:, t.slot(s, "b")], ring[:, t.slot(s, "c")]
                    done_before = t.k * (4 * (NS - 1)) + (l + u + (1 if l else 0)) * (NS - 1)
                    with pe.Fori(1, NS) as n:
                        pe.wait_ge(sem("gen_weights"), done_before + n)
                        for o, k in ((ob, 0), (oc, 1)):
                            for b in range(NBANK[l]):
                                ins = mm(o[:, b, 0:COLS], gen_w[:, k], xs[l][u][:, b * COLS:(b + 1) * COLS],
                                         start=True, stop=True)
                        ins.then_inc(sem("gen_bc"), 1)
                    need(pe, t, f"dve {s}", "carry")

            walk(pe, do)
            pe.wait_ge(sem("flag_sum"), 1)
            need_all = done["act ffn"]
            pe.wait_ge(need_all, NG * len(STEPS["act ffn"]))
            mm(ring[0:1, 0, 0, 0:1], flag_sum[:], blk_mean[:, 0:1], start=True, stop=False, skip_group_check=True)
            mm(ring[0:1, 0, 0, 0:1], flag_sum[:], blk_mean[:, E:E + 1], start=False, stop=True,
               skip_group_check=True).then_inc(sem("flag_pe"), 1)
            pe.wait_ge(prep["flag"], 1)
            again = pe.value_load(flag_i[0:1, 0:1], min_val=0, max_val=1)
            with pe.If(again != 0):
                walk_general(pe, do_general)

        @block.vector
        def _(dve):
            v = nc.vector
            made = prep["const"]
            tt, ts, stt = v.tensor_tensor, v.tensor_scalar, v.scalar_tensor_tensor

            v.memset(rw1[:], 0.0).then_inc(made, 1)
            v.memset(rw2[:], 0.0).then_inc(made, 1)
            v.memset(w2[:], 0.0).then_inc(made, 1)
            v.memset(b3[:], 0.0).then_inc(made, 1)
            v.memset(wp_in[:], 0.0).then_inc(made, 1)
            for t_, val in ((blk, 1.0), (blk_half, 0.5), (blk_mean, 1.0 / E)):
                v.memset(t_[:], 0.0).then_inc(made, 1)
            for t_ in (wq_bd, wk_bd, wv_bd):
                v.memset(t_[:], 0.0).then_inc(made, 1)
            dve.wait_ge(made, 11)
            for t_, val in ((blk, 1.0), (blk_half, 0.5), (blk_mean, 1.0 / E)):
                for k in range(2):
                    half = slice(E * k, E * k + E)
                    v.memset(t_[half, half], val).then_inc(made, 1)
            for t_, val in ((four, 4.0), (zero_col, 0.0), (clamp_col, CLAMP), (under_col, -UNDERFLOW),
                            (two_col, 2.0), (ln_col, 12.0 * LN2), (eps_col, LN_EPS), (v1, 0.0), (gate_part, 0.0)):
                v.memset(t_[:], val).then_inc(made, 1)
            for e in range(NX):
                v.memset(rank[:, :, e:e + 1], float(NX - e)).then_inc(made, 1)
            cleared = [t_[u] for l in range(LAYERS) for t_ in (dec[l], vin[l]) for u in range(UNITS[l])]
            for t_ in cleared:
                v.memset(t_[:], 0.0).then_inc(made, 1)
            for pb in pm:
                for t_ in pb:
                    v.memset(t_[:], 0.0).then_inc(made, 1)
            consts = 11 + 6 + 9 + NX + len(cleared) + 4
            dve.wait_ge(made, consts)
            for t_ in (pm[0][0], pm[0][1], pm[1][0], pm[1][1]):
                v.memset(t_[KROW:KROW + 1], 1.0).then_inc(made, 1)
            v.memset(v1[0:TOUT, :, :, 0:1], 1.0).then_inc(made, 1)
            dve.wait_ge(made, consts + 5)

            dve.wait_ge(prep["dma"], 16 * NPREP)
            dve.wait_ge(sem("masks"), MASKS)
            dve.wait_ge(prep["pe"], 4)
            dve.wait_ge(prep["exp"], 1)
            c = prep["copy"]
            n = 0
            for l in range(LAYERS):
                o = ring[:, l, 0]
                tt(m_quad[:, l], o[:, 0:P], blk[:], ALU.mult).then_inc(c, 1)
                tt(m_delta[:, l], o[:, P:2 * P], blk[:], ALU.mult).then_inc(c, 1)
                v.tensor_copy(wT[:, l], o[:, 2 * P:3 * P]).then_inc(c, 1)
                ts(decay[:, l], decay[:, l], -1.0, None, ALU.mult).then_inc(c, 1)
                ts(nbdt_col[:, l:l + 1], bdt_col[:, l:l + 1], -1.0, CLAMP, ALU.mult, ALU.add).then_inc(c, 1)
                n += 5
            for b in range(2):
                v.tensor_copy(wp_t[:, b], ring[:, 3, 0, P + E * (b + 1):P + E * (b + 2)]).then_inc(c, 1)
            v.tensor_copy(b3_part[0][:], b3[:]).then_inc(c, 1)
            n += 3
            for t_, at in ((wq_bd, 0), (wk_bd, E), (wv_bd, P)):
                for k in range(2):
                    half = slice(E * k, E * k + E)
                    v.tensor_copy(t_[half, half], ring[half, 3, 0, at:at + E]).then_inc(c, 1)
                    n += 1
            v.tensor_reduce(mask_q[:], head16[:].rearrange("p (a j) -> p j a", j=4), AX_X, ALU.add).then_inc(c, 1)
            n += 1
            dve.wait_ge(c, n)
            for l in range(LAYERS):
                scale = 0.5 if l < LAYERS - 1 else 1.0
                ts(m_b0[:, l], blk[:], wT[:, l, 0:1], None, ALU.mult).then_inc(c, 1)
                ts(m_c0[:, l], blk[:], wT[:, l, NS:NS + 1], scale, ALU.mult, ALU.mult).then_inc(c, 1)
                v.tensor_reduce(decay_max[:, l:l + 1], decay[:, l, 1:NS], AX_X, ALU.max).then_inc(c, 1)
                ts(d_col[:, l:l + 1], d_col[:, l:l + 1], scale, None, ALU.mult).then_inc(c, 1)
                n += 4
            ts(mask_q[:], mask_q[:], temp_col[:, 0:1], SCALE2, ALU.mult, ALU.mult).then_inc(c, 1)
            tt(b3_rest[:], b3[:], b3_part[0][:], ALU.subtract).then_inc(c, 1)
            dve.wait_ge(c, n + 2)
            v.tensor_copy(b3_part[1][:], b3_rest[:]).then_inc(c, 1)
            dve.wait_ge(c, n + 3)
            tt(b3_part[2][:], b3_rest[:], b3_part[1][:], ALU.subtract).then_inc(c, 1)
            dve.wait_ge(c, n + 4)
            v.memset(zero_col[:], 0.0).then_inc(prep["done"], 1)

            def ssm(t, s, ph, general=False):
                l, u = layer_unit(s)
                nb = NBANK[l]
                me = done[f"dve {s}"]
                X, W = banks(xs[l][u][:], nb), nb * COLS

                def made_by(job):
                    need(dve, t, f"pe {s}", job)
                    return ring[:, t.slot(s, job), 0:nb, 0:COLS]

                if ph == 1:
                    o = made_by("dpre")
                    need(dve, t, f"act {s}", "ln")
                    stt(banks(delta[l][u][:], nb), o, bdt_col[:, l:l + 1], banks(soft[l][u][:], nb),
                        ALU.add, ALU.max).then_inc(me, 1)
                if ph == 2:
                    o = made_by("z")
                    need(dve, t, f"dve {s}", "delta")
                    tt(banks(soft[l][u][:], nb), o, X, ALU.mult).then_inc(me, 1)
                if ph == 3:
                    o = made_by("b")
                    need(dve, t, f"pool {s}", "du")
                    tt(banks(vin[l][u][:, 1:W + 1], nb), o, banks(du[l][u][:], nb), ALU.mult).then_inc(me, 1)
                    need(dve, t, f"dve {s}", "vin")
                    need(dve, t, f"act {s}", "decay")
                    need(dve, t, f"pool {s}", STEPS[f"pool {s}"][-1], back=1)
                    v.tensor_tensor_scan(carry[l][u][:], vin[l][u][:, 0:W], dec[l][u][:], 0.0,
                                         ALU.add, ALU.mult).then_inc(me, 1)
                if ph == 4:
                    o = made_by("s")
                    tt(banks(base[l][u][:], nb), o, banks(du[l][u][:], nb), ALU.mult).then_inc(me, 1)
                    need(dve, t, f"dve {s}", "base")
                    stt(base[l][u][:], xs[l][u][:], d_col[:, l:l + 1], base[l][u][:],
                        ALU.mult, ALU.add).then_inc(me, 1)
                if ph == 5:
                    o = made_by("c")
                    need(dve, t, f"dve {s}", "scan")
                    tt(banks(carry[l][u][:], nb), o, banks(carry[l][u][:], nb), ALU.mult).then_inc(
                        sem("gen_first") if general else me, 1)

            def norm(t, s, ph, h):
                w, me = s[0], done[f"dve {s}"]
                if ph == 0:
                    need(dve, t, f"pe {s}", "mean")
                    tt(cen[w][:], h[:], ring[:, t.slot(s, "mean"), 0, 0:COLS], ALU.subtract).then_inc(me, 1)
                if ph == 1:
                    need(dve, t, f"act {s}", "rstd")
                    need(dve, t, f"pe {s}", "v" if w == "a" else f"h1_{NEP - 1}", back=1)
                    tt(nrm[w][:], cen[w][:], rstd[w][:], ALU.mult).then_inc(me, 1)

            def attention(t, s, ph):
                norm(t, s, ph, h_in)
                me = done["dve att"]
                if ph == 2:
                    need(dve, t, "pe att", "qk")
                    need(dve, t, "pe att", "s31", back=1)
                    need(dve, t, "pool att", "qe", back=1)
                    for b in range(2):
                        ts(qk[:, b], ring[:, t.slot(s, "qk"), b, 0:COLS], bqk_col[:, b:b + 1], None,
                           ALU.add).then_inc(me, 1)
                if ph == 3:
                    need(dve, t, "pe att", "n2")
                    for b, eps in ((0, NORM_EPS ** 2 / SCALE2), (1, NORM_EPS ** 2)):
                        ts(qk_sq[:, b], ring[:, t.slot(s, "n2"), b, 0:COLS], eps, None,
                           ALU.max).then_inc(me, 1)
                    need(dve, t, "act att", "rnorm")
                    tt(qk[:], qk[:], qk_sq[:], ALU.mult).then_inc(me, 1)
                if ph == 4:
                    need(dve, t, "pe att", "v")
                    need(dve, t, "pe att", "y3", back=1)
                    src = ring[0:TOUT, t.slot(s, "v"), 0, :].rearrange("m (q h d) -> m q h d", q=NPAIR, d=HD)
                    bias = bv_row[:].rearrange("m k (h d) -> m (k h) d", d=HD)[:, None, :, :].broadcast_to(
                        [TOUT, NPAIR, 2 * H, HD])
                    tt(v1[0:TOUT, :, :, 1:HD + 1], src, bias, ALU.add).then_inc(me, 1)
                if 7 <= ph <= 10:
                    q = ph - 7
                    need(dve, t, "act att", f"rec{q}")
                    need(dve, t, "pe att", "proj", back=1)
                    tt(attT[:, q].rearrange("p a n -> p (a n)"), yT[q % 2][:], y_rec[q % 2][:],
                       ALU.mult).then_inc(me, 1)
                if ph == LASTP:
                    need(dve, t, "pe att", "proj")
                    need(dve, t, "dve ffn", "fin", group=t.group(s) - 1)
                    stt(h_mid[:], ring[:, t.slot(s, "proj"), 0, 0:COLS], bp_col[:, 0:1], h_in[:],
                        ALU.add, ALU.add).then_inc(me, 1)

            def spread(col):
                return col[:, :, None].broadcast_to([TOUT, GB, NX])

            def experts(t, s, ph):
                norm(t, s, ph, h_mid)
                me = done["dve ffn"]

                def step(ins, name):
                    ins.then_inc(me, 1)
                    need(dve, t, "dve ffn", name)

                if ph == 3:
                    need(dve, t, "pe ffn", "lg")
                    src = ring[0:TOUT, t.slot(s, "lg"), 0, 0:GB * NX].rearrange("m (b e) -> m b e", e=NX)
                    step(tt(lg[:], src, rb2_row[:, None, :].broadcast_to([TOUT, GB, NX]), ALU.add), "lg")
                    step(v.tensor_reduce(st[:, 0], lg[:], AX_X, ALU.max), "mx")
                    step(tt(lg[:], lg[:], spread(st[:, 0]), ALU.subtract), "shift")
                    need(dve, t, "act ffn", "prexp")
                    step(v.tensor_reduce(st[:, 1], pr[:], AX_X, ALU.add), "sum")
                    step(v.reciprocal(st[:, 2], st[:, 1]), "rsum")
                    step(tt(pr[:], pr[:], spread(st[:, 2]), ALU.mult), "pr")
                if ph in (4, 5):
                    k = ph - 4
                    m = st[:, 3 + k]
                    step(v.tensor_reduce(m, pr[:], AX_X, ALU.max), f"m{k}")
                    step(tt(key[:], pr[:], spread(m), ALU.is_ge), f"eq{k}")
                    step(tt(key[:], key[:], rank[:], ALU.mult), f"key{k}")
                    step(v.tensor_reduce(st[:, 7], key[:], AX_X, ALU.max), f"kmax{k}")
                    step(tt(oh[k][:], key[:], spread(st[:, 7]), ALU.is_equal), f"oh{k}")
                if ph == 4:
                    step(stt(pr[:], oh[0][:], -4.0, pr[:], ALU.mult, ALU.add), "rest")
                if ph == 5:
                    step(tt(st[:, 5], st[:, 4], st[:, 3], ALU.subtract), "diff")
                    need(dve, t, "act ffn", "topexp")
                    step(ts(st[:, 0], st[:, 6], 1.0, None, ALU.add), "den")
                    step(v.reciprocal(st[:, 1], st[:, 0]), "r0")
                    step(tt(st[:, 2], st[:, 1], st[:, 6], ALU.mult), "r1")
                    need(dve, t, "pool ffn", "lo", back=1)
                    step(tt(oh[0][:], oh[0][:], spread(st[:, 1]), ALU.mult), "g0")
                    step(tt(oh[1][:], oh[1][:], spread(st[:, 2]), ALU.mult), "g1")
                    step(tt(gate[:], oh[0][:], oh[1][:], ALU.add), "gate")
                k = ph - 7
                if 0 <= k < NEP:
                    need(dve, t, "pe ffn", f"g_{k}")
                    need(dve, t, "act ffn", f"hid2_{k}")
                    tt(hidw[k][:], hid2[:], ring[:, t.slot(s, f"g_{k}"), :, 0:COLS], ALU.mult).then_inc(me, 1)

                if ph == 10:
                    need(dve, t, "pe ffn", "o")
                    need(dve, t, "pe ffn", "oT", back=1)
                    tt(fin[:], ring[:, t.slot(s, "o"), 0, 0:COLS], h_mid[:], ALU.add).then_inc(me, 1)

            def do(t, s, ph):
                {"L": ssm, "a": attention, "f": experts}[s[0]](t, s, ph)

            def do_general(t, s, ph):
                if s[0] == "L":
                    ssm(t, s, ph, general=True)
                else:
                    do(t, s, ph)
                if s[0] == "L" and ph == 5:
                    l, u = layer_unit(s)
                    nb, W = NBANK[l], NBANK[l] * COLS
                    scale = 0.5 if l < LAYERS - 1 else 1.0
                    done_before = t.k * (4 * (NS - 1)) + (l + u + (1 if l else 0)) * (NS - 1)
                    ob = ring[:, t.slot(s, "b"), 0:nb, 0:COLS]
                    oc = ring[:, t.slot(s, "c"), 0:nb, 0:COLS]
                    q, w = sem("gen_w_steps"), sem("gen_steps")
                    with dve.Fori(1, NS) as n:
                        at = done_before + n - 1
                        ts(gen_w[:, 0], blk[:], wT[:, l, bass.ds(n, 1)], None, ALU.mult).then_inc(q, 1)
                        ts(gen_w[:, 1], blk[:], wT[:, l, bass.ds(n + NS, 1)], scale, ALU.mult, ALU.mult).then_inc(q, 1)
                        dve.wait_ge(q, at * 2 + 2)
                        v.tensor_copy(gen_a[:], decay[:, l, bass.ds(n, 1)]).then_inc(sem("gen_weights"), 1)
                        dve.wait_ge(sem("gen_bc"), at + 1)
                        dve.wait_ge(sem("gen_decay"), at + 1)
                        tt(banks(vin[l][u][:, 1:W + 1], nb), ob, banks(du[l][u][:], nb), ALU.mult).then_inc(w, 1)
                        dve.wait_ge(w, at * 4 + 1)
                        v.tensor_tensor_scan(soft[l][u][:], vin[l][u][:, 0:W], dec[l][u][:], 0.0,
                                             ALU.add, ALU.mult).then_inc(w, 1)
                        dve.wait_ge(w, at * 4 + 2)
                        tt(banks(soft[l][u][:], nb), oc, banks(soft[l][u][:], nb), ALU.mult).then_inc(w, 1)
                        dve.wait_ge(w, at * 4 + 3)
                        tt(carry[l][u][:], carry[l][u][:], soft[l][u][:], ALU.add).then_inc(w, 1)
                        dve.wait_ge(w, at * 4 + 4)
                    v.memset(zero_col[:], 0.0).then_inc(done[f"dve {s}"], 1)

            walk(dve, do)
            for s in ("L0u0", "L0u1", "L1", "L2"):
                dve.wait_ge(done[f"pool {s}"], NG * len(STEPS[f"pool {s}"]))
            v.tensor_reduce(flag_sum[:], flags[:], AX_X, ALU.add).then_inc(sem("flag_sum"), 1)
            dve.wait_ge(sem("flag_pe"), 1)
            ts(flag_i[:], ring[0:1, 0, 0, 0:1], 0.0, None, ALU.is_gt).then_inc(prep["flag"], 1)
            dve.wait_ge(prep["flag"], 1)
            again = dve.value_load(flag_i[0:1, 0:1], min_val=0, max_val=1)
            with dve.If(again != 0):
                walk_general(dve, do_general)


_INS = ["x", "L0_tok_A_log", "L0_tok_D", "L0_tok_W_dbc", "L0_tok_W_dt", "L0_tok_b_dt", "L0_attn_Wqkv",
        "L0_attn_bqkv", "L0_attn_Wproj", "L0_attn_bproj", "L0_attn_temperature", "L0_ffn_router_w1",
        "L0_ffn_router_b1", "L0_ffn_router_w2", "L0_ffn_router_b2", "L0_ffn_expert_w1", "L0_ffn_expert_b1",
        "L0_ffn_expert_w2", "L0_ffn_expert_b2", "L0_ffn_expert_w3", "L0_ffn_expert_b3"]
_OUTS = [((128, 93, 64), "float32")]


def kernel(**inputs):
    import numpy as _np
    import concourse.bacc as _bacc
    from concourse import mybir as _mybir
    from concourse.bass_utils import run_bass_kernel_spmd as _run

    nc = _bacc.Bacc("TRN2", target_bir_lowering=False, num_devices=1)
    arrays, args = {}, []
    for name in _INS:
        a = _np.ascontiguousarray(inputs[name])
        arrays[f"in_{name}_dram"] = a
        args.append(nc.dram_tensor(f"in_{name}_dram", a.shape, _mybir.dt.from_np(a.dtype), kind="ExternalInput").ap())
    for i, (shape, dtype) in enumerate(_OUTS):
        dt = _mybir.dt.from_np(_np.dtype(dtype))
        args.append(nc.dram_tensor(f"out_{i}_dram", shape, dt, kind="ExternalOutput").ap())
    audio_tower(nc, *args)
    r = _run(nc, [arrays], core_ids=[0])
    got = tuple(r.results[0][f"out_{i}_dram"] for i in range(len(_OUTS)))
    return got[0]
```
